# Optimizing a Trainium2 kernel written in Bass

```python
import numpy as np
import jax
import jax.numpy as jnp

def _softmax(x, axis=-1):
    return jax.nn.softmax(x, axis=axis)

def _gelu(x):
    return jax.nn.gelu(x, approximate=True)

def _silu(x):
    return jax.nn.silu(x)

def _sigmoid(x):
    return jax.nn.sigmoid(x)

def _layernorm(x, axis=-1, eps=1e-05):
    m = jnp.mean(x, axis=axis, keepdims=True)
    v = jnp.var(x, axis=axis, keepdims=True)
    return (x - m) / jnp.sqrt(v + eps)

def _scatter_add(tgt, idx, src, axis=0):
    return tgt.at[idx].add(src)

def _segment_sum(src, seg, n):
    return jax.ops.segment_sum(src, seg, n)
kernel_name = 'mk_gnn_ffn_d1_gnn_r8_9e77bf'

def setup_inputs(seed: int=0):
    np.random.seed(seed)
    _w = jnp.asarray

    def _rec_inputs():
        import jax
        import jax.numpy as jnp
        _gk = jax.random.key(seed)
        x = -8.776e-05 + 1 * jax.random.normal(jax.random.fold_in(_gk, 1), (6250, 256), jnp.float32)
        src = jax.random.randint(jax.random.fold_in(_gk, 2), (100000,), 0, 6250, jnp.int32)
        dst = jax.random.randint(jax.random.fold_in(_gk, 3), (100000,), 0, 6250, jnp.int32)
        _o = jnp.argsort(dst, stable=True)
        src = src[_o]
        dst = dst[_o]
        edge_type_16 = jax.random.randint(jax.random.fold_in(_gk, 12), (100000,), 0, 16, jnp.int32)
        edge_weight1 = jax.random.uniform(jax.random.fold_in(_gk, 13), (100000, 1), jnp.float32, 0.0, 0.999998)
        return (x, src, dst, edge_type_16, edge_weight1)
    x, src, dst, edge_type_16, edge_weight1 = _rec_inputs()

    def _L0_gnn_setup():
        import jax, jax.numpy as jnp
        import numpy as np
        N_NODES = 2500
        N_EDGES = 40000
        NUM_RELS = 16
        IN_FEAT = 256
        OUT_FEAT = 256
        key = jax.random.key(seed)
        k_h, k_w, k_n, k_s, k_d, k_r = jax.random.split(key, 6)
        h = jax.random.normal(k_h, (N_NODES, IN_FEAT), dtype=jnp.float32)
        weight = jax.random.normal(k_w, (NUM_RELS, IN_FEAT, OUT_FEAT), dtype=jnp.float32)
        norm = jax.random.uniform(k_n, (N_EDGES, 1), dtype=jnp.float32)
        src = jax.random.randint(k_s, (N_EDGES,), 0, N_NODES, dtype=jnp.int32)
        dst = jax.random.randint(k_d, (N_EDGES,), 0, N_NODES, dtype=jnp.int32)
        rel_type = jax.random.randint(k_r, (N_EDGES,), 0, NUM_RELS, dtype=jnp.int32)
        return {'h': h, 'weight': weight, 'norm': norm, 'src': src, 'dst': dst, 'rel_type': rel_type}
    _L0_gnn_all = _L0_gnn_setup()
    _L0_gnn_in = {k: v for k, v in _L0_gnn_all.items() if k in ('weight',)}
    del _L0_gnn_all

    def _L0_ffn_setup():
        import jax, jax.numpy as jnp
        import numpy as np
        N_EXPERTS = 8
        TOP_K = 2
        key = jax.random.key(seed)
        ks = jax.random.split(key, 5)
        B, T, C, E, H = (8, 256, 256, 8, 682)
        scale = 1.0 / np.sqrt(C)
        return {'x': jax.random.normal(ks[0], (B, T, C), dtype=jnp.float32), 'router_w': jax.random.normal(ks[1], (E, C), dtype=jnp.float32) * scale, 'w1': jax.random.normal(ks[2], (E, H, C), dtype=jnp.float32) * scale, 'w2': jax.random.normal(ks[3], (E, C, H), dtype=jnp.float32) * (1.0 / np.sqrt(H)), 'w3': jax.random.normal(ks[4], (E, H, C), dtype=jnp.float32) * scale}
    _L0_ffn_all = _L0_ffn_setup()
    _L0_ffn_in = {k: v for k, v in _L0_ffn_all.items() if k in ('router_w', 'w1', 'w2', 'w3')}
    del _L0_ffn_all
    return {'x': x, 'src': src, 'dst': dst, 'edge_type_16': edge_type_16, 'edge_weight1': edge_weight1, 'L0_gnn_weight': _L0_gnn_in['weight'], 'L0_ffn_router_w': _L0_ffn_in['router_w'], 'L0_ffn_w1': _L0_ffn_in['w1'], 'L0_ffn_w2': _L0_ffn_in['w2'], 'L0_ffn_w3': _L0_ffn_in['w3']}

def reference(x, src, dst, edge_type_16, edge_weight1, L0_gnn_weight, L0_ffn_router_w, L0_ffn_w1, L0_ffn_w2, L0_ffn_w3):
    import jax
    import jax.numpy as jnp

    def _L0_gnn_ref(h, weight, norm, src, dst, rel_type):
        import jax, jax.numpy as jnp
        import numpy as np
        N_NODES = 2500
        N_EDGES = 40000
        NUM_RELS = 16
        IN_FEAT = 256
        OUT_FEAT = 256
        transformed = jnp.einsum('ni,rio->rno', h, weight)
        msg = transformed[rel_type, src] * norm
        out = jax.ops.segment_sum(msg, dst, num_segments=h.shape[0])
        return out

    def _L0_ffn_ref(x, router_w, w1, w2, w3):
        import jax, jax.numpy as jnp
        import numpy as np
        N_EXPERTS = 8
        TOP_K = 2
        B, T, C = x.shape
        flat = x.reshape(-1, C)
        logits = flat @ router_w.T
        probs = jax.nn.softmax(logits, axis=-1)
        topk_probs, topk_idx = jax.lax.top_k(probs, TOP_K)
        topk_probs = topk_probs / (jnp.sum(topk_probs, axis=-1, keepdims=True) + 1e-09)
        onehot = jax.nn.one_hot(topk_idx, N_EXPERTS, dtype=flat.dtype)
        gates = jnp.einsum('nk,nke->ne', topk_probs, onehot)
        h1 = jnp.einsum('nc,ehc->neh', flat, w1)
        h3 = jnp.einsum('nc,ehc->neh', flat, w3)
        h = jax.nn.silu(h1) * h3
        y = jnp.einsum('neh,ech->nec', h, w2)
        out = jnp.einsum('ne,nec->nc', gates, y)
        return out.reshape(B, T, C)
    x = x + _L0_gnn_ref(_layernorm(x, axis=-1), L0_gnn_weight, edge_weight1, src, dst, edge_type_16)
    x = x + _L0_ffn_ref(_layernorm(x, axis=-1)[None], L0_ffn_router_w, L0_ffn_w1, L0_ffn_w2, L0_ffn_w3)[0]
    return x

_drawn_inputs = setup_inputs


def setup_inputs(seed=0):
    import zlib

    import numpy as np

    out = dict(_drawn_inputs(seed))
    spreads = {}
    factors = {'L0_ffn_router_w': 5.306, 'L0_ffn_w1': 5.0, 'L0_ffn_w2': 4.673, 'L0_ffn_w3': 4.672}
    for name, (base, spread) in spreads.items():
        noise = np.random.default_rng([zlib.crc32(name.encode()), seed]).standard_normal(out[name].shape)
        drawn = base * np.exp(spread * noise) if base else spread * noise
        out[name] = jnp.asarray(drawn.astype(out[name].dtype))
    for name, factor in factors.items():
        out[name] = (out[name] * factor).astype(out[name].dtype)
    return out
```

```python
from contextlib import ExitStack

import concourse.bass as bass
from concourse import mybir

F32 = mybir.dt.float32
F16 = mybir.dt.float16
I32 = mybir.dt.int32
U32 = mybir.dt.uint32
ALU = mybir.AluOpType
ACT = mybir.ActivationFunctionType
AX = mybir.AxisListType
RMAX = bass.bass_isa.ReduceOp.max
ds = bass.ds

P = 128
N_NODES, C = 6250, 256
N_EDGES = 100000
N_RELS = 16
N_EXP, H = 8, 682
KC = C // P
NT = -(-N_NODES // P)
LAST = N_NODES - (NT - 1) * P
NPAD = NT * P
EPS = 1e-5

EPT = 8
CHUNK = EPT * P
NCH = 2 * -(-N_EDGES // (2 * CHUNK))

TOK = 256
NJ = (2 * N_NODES + N_EXP * (TOK - 1)) // TOK
SLOTS = NJ * TOK
HM = H // P
HT = H - HM * P
NM = HM + 1
W13 = (2 * HM + 1) * P
W2 = NM * C
W_HI13, W_LO13 = 0, KC * W13
W_HI2, W_LO2 = 2 * KC * W13, 2 * KC * W13 + W2
WPE = 2 * KC * W13 + 2 * W2
HSCALE = 1.0 / 16
assert NJ % 2 == 0 and NT % 2 == 1 and HT <= 64


def chained(eng, sem):
    count = [0]

    def link(ins):
        count[0] += 1
        ins.then_inc(sem, 1)
        eng.wait_ge(sem, count[0])
    return link


def row_stats(nc, link, stats, mean, var, tmp):
    v = nc.vector
    me, m2e, mo, m2o = stats[:, :, 1], stats[:, :, 2], stats[:, :, 4], stats[:, :, 5]
    link(v.tensor_tensor(tmp[:, :], me, mo, ALU.subtract))
    link(v.tensor_tensor(mean[:, :], me, mo, ALU.add))
    link(v.tensor_tensor(var[:, :], m2e, m2o, ALU.add))
    link(v.tensor_tensor(tmp[:, :], tmp[:, :], tmp[:, :], ALU.mult))
    link(v.tensor_scalar(mean[:, :], mean[:, :], 0.5, None, ALU.mult))
    link(v.tensor_scalar(var[:, :], var[:, :], 1.0 / C, EPS, ALU.mult, ALU.add))
    link(v.scalar_tensor_tensor(out=var[:, :], in0=tmp[:, :], scalar=0.25, in1=var[:, :],
                                op0=ALU.mult, op1=ALU.add))


def constants(nc, ctx):
    def sb(name, shape, dt=F32):
        return ctx.enter_context(nc.sbuf_tensor(name, shape, dt))
    c = {
        "ident": sb("ident", [P, P]),
        "lower": sb("lower", [P, P], F16),
        "ones": sb("ones", [P, P], F16),
        "node_id": sb("node_id", [P, P]),
        "tile_base": sb("tile_base", [P, NT]),
        "first_wins": sb("first_wins", [P, N_EXP]),
        "slot_tile": sb("slot_tile", [P, NJ]),
        "valid": sb("valid", [P, NT]),
    }
    made = ctx.enter_context(nc.semaphore("const_made"))
    cleared = ctx.enter_context(nc.semaphore("const_cleared"))
    with nc.Block() as block:
        @block.gpsimd
        def _(pool):
            g = nc.gpsimd
            g.memset(c["ident"][:, :], 0.0).then_inc(cleared, 1)
            g.memset(c["lower"][:, :], 0.0).then_inc(cleared, 1)
            g.memset(c["valid"][:, :], 1.0).then_inc(cleared, 1)
            g.memset(c["ones"][:, :], 1.0).then_inc(made, 1)
            opts = dict(channel_multiplier=0, allow_small_or_imprecise_dtypes=True)
            g.iota(c["node_id"][:, :], pattern=[[1, P]], base=0, **opts).then_inc(made, 1)
            g.iota(c["tile_base"][:, :], pattern=[[P, NT]], base=0, **opts).then_inc(made, 1)
            g.iota(c["first_wins"][:, :], pattern=[[-1, N_EXP]], base=N_EXP, **opts).then_inc(made, 1)
            g.iota(c["slot_tile"][:, :], pattern=[[1, NJ]], base=0, **opts).then_inc(made, 1)
            pool.wait_ge(cleared, 3)
            g.affine_select(out=c["ident"][:, :], in_=c["ident"][:, :], compare_op=ALU.not_equal,
                            fill=1.0, base=0, pattern=[[-1, P]], channel_multiplier=1).then_inc(made, 1)
            g.affine_select(out=c["lower"][:, :], in_=c["lower"][:, :], compare_op=ALU.is_ge,
                            fill=1.0, base=0, pattern=[[-1, P]], channel_multiplier=1).then_inc(made, 1)
            g.affine_select(out=c["valid"][:, :], in_=c["valid"][:, :], compare_op=ALU.is_ge,
                            fill=0.0, base=N_NODES - 1, pattern=[[-P, NT]],
                            channel_multiplier=-1).then_inc(made, 1)
            pool.wait_ge(made, 8)
    return c


def transform(nc, cst, x_rows, edges, x_in, gw, src, dst, rel, norm, table):
    ctx = ExitStack()
    with ctx:
        def sb(name, shape, dt=F32):
            return ctx.enter_context(nc.sbuf_tensor(name, shape, dt))

        def sem(name):
            return ctx.enter_context(nc.semaphore(name))

        wst = sb("w_stage", [P, KC, N_RELS * C])
        whi = sb("w_hi", [P, KC, N_RELS * C], F16)
        wlo = sb("w_lo", [P, KC, N_RELS * C], F16)
        stage = [sb(f"row_stage{b}", [P, N_RELS * C]) for b in range(2)]
        normed = [sb(f"normed{b}", [P, C]) for b in range(2)]
        xhi = [sb(f"x_hi{b}", [P, KC, P], F16) for b in range(2)]
        xlo = [sb(f"x_lo{b}", [P, KC, P], F16) for b in range(2)]
        stats = sb("ln_stats", [P, NT, 6])
        mean, var, tmp = sb("ln_mean", [P, NT]), sb("ln_var", [P, NT]), sb("ln_tmp", [P, NT])
        srci = sb("src_i", [P, NCH * EPT], I32)
        reli = sb("rel_i", [P, NCH * EPT], I32)
        dsti = sb("dst_i", [P, NCH * EPT], I32)
        ends = sb("chunk_ends", [P, 2 * NCH])
        ends_all = sb("chunk_ends_all", [P, 2 * NCH])
        endi = sb("chunk_ends_i", [P, 2 * NCH], I32)
        endf = sb("chunk_ends_f", [P, 2 * NCH])
        steps = sb("chunk_steps", [P, NCH])
        ones_row = sb("ones_row", [P, NCH])
        stepsum = sb("chunk_stepsum", [P, NCH])
        tp = [ctx.enter_context(nc.psum_tensor(f"xT{b}", [P, 512], F32)) for b in range(2)]
        out4 = [ctx.enter_context(nc.psum_tensor(f"rel_out{b}", [P, 512], F32)) for b in range(4)]

        x_loaded = [sem(f"x_loaded{g}") for g in range(7)]
        w_loaded = [sem(f"w_loaded{k}") for k in range(KC)]
        e_loaded = sem("edges_loaded")
        w_hi_done, w_lo_done = sem("w_hi_done"), sem("w_lo_done")
        chain, sqrt_in, sqrt_done = sem("a_chain"), sem("sqrt_in"), sem("sqrt_done")
        normed_ready, transposed = sem("normed_ready"), sem("x_transposed")
        hi_ready, lo_ready = sem("x_hi_ready"), sem("x_lo_ready")
        group_done, even_out, odd_out = sem("group_done"), sem("even_out"), sem("odd_out")
        stored = [sem(f"rows_stored{b}") for b in range(2)]
        ends_in, ends_out = sem("chunk_ends_in"), sem("chunk_ends_out")

        x_v = x_in.rearrange("(t p) c -> p t c", p=P)
        gw_v = gw.rearrange("r (k p) o -> k p r o", p=P)
        table_v = table.rearrange("(r t p) c -> t p r c", r=N_RELS, p=P)
        TG = NT // 7
        W4 = N_RELS * C // 4

        def over_tiles(eng, body):
            body(0, 0, 0, 2)
            with eng.Fori(0, (NT - 3) // 2) as i:
                body(2 * i + 1, i, 1, 2)
                body(2 * i + 2, i + 1, 0, 2)
            body(NT - 2, (NT - 2) // 2, (NT - 2) % 2, 1)
            body(NT - 1, (NT - 1) // 2, (NT - 1) % 2, 0)

        def first(t, n=1):
            return isinstance(t, int) and t < n

        with nc.Block() as block:
            @block.sync
            def _(sp):
                for k in range(KC):
                    sp.dma_start(wst[:, k, :].rearrange("p (r o) -> p r o", r=N_RELS),
                                 gw_v[k]).then_inc(w_loaded[k], 16)

                def body(t, half, b, follow):
                    sp.wait_ge(even_out, 4 * t + 4)
                    sp.wait_ge(odd_out, 4 * t + 4)
                    sp.dma_start(table_v[ds(t, 1)].rearrange("a p r c -> p (a r) c"),
                                 stage[b][:, :].rearrange("p (r c) -> p r c", r=N_RELS)).then_inc(stored[b], 16)
                over_tiles(sp, body)
                sp.wait_ge(stored[0], 16 * ((NT + 1) // 2))
                sp.wait_ge(stored[1], 16 * (NT // 2))

            @block.gpsimd
            def _(pool):
                pool.wait_ge(ends_in, 1)
                nc.gpsimd.partition_all_reduce(ends_all[:, :], ends[:, :], P, RMAX).then_inc(ends_out, 1)
                pool.wait_ge(ends_out, 1)

            @block.scalar
            def _(act):
                for g in range(7):
                    act.dma_start(x_rows[:, g * TG:(g + 1) * TG, :],
                                  x_v[:, g * TG:(g + 1) * TG, :]).then_inc(x_loaded[g], 16)
                for to, of in ((srci, src), (reli, rel), (dsti, dst), (edges["norm"], norm)):
                    act.dma_start(to[:, :], of).then_inc(e_loaded, 16)
                for k in range(KC):
                    act.wait_ge(w_loaded[k], 16)
                    for q in range(4):
                        s = slice(q * W4, (q + 1) * W4)
                        nc.scalar.activation(whi[:, k, s], wst[:, k, s], ACT.Copy).then_inc(w_hi_done, 1)
                act.wait_ge(sqrt_in, 1)
                nc.scalar.activation(var[:, :], var[:, :], ACT.Sqrt).then_inc(sqrt_done, 1)

                def high(t, b):
                    act.wait_ge(transposed, t + 1)
                    if not first(t, 2):
                        act.wait_ge(group_done, 8 * t - 8)
                    nc.scalar.activation(xhi[b][:, :, :], tp[b][:, 0:C].rearrange("p (k n) -> p k n", k=KC),
                                         ACT.Copy).then_inc(hi_ready, 1)

                def body(t, half, b, follow):
                    if follow >= 1:
                        high(t + 1, 1 - b)
                    for g in (0, 2, 4, 6):
                        act.wait_ge(group_done, 8 * t + g + 1)
                        if g == 0 and not first(t, 2):
                            act.wait_ge(stored[b], 16 * half)
                        nc.scalar.activation(stage[b][:, g * 512:(g + 1) * 512], out4[g % 4][:, :],
                                             ACT.Copy).then_inc(even_out, 1)
                high(0, 0)
                over_tiles(act, body)

            @block.vector
            def _(dve):
                v = nc.vector
                link = chained(dve, chain)
                for g in range(7):
                    dve.wait_ge(x_loaded[g], 16)
                    for t in range(g * TG, (g + 1) * TG):
                        last = v.bn_stats(stats[:, t, :], x_rows[:, t, :])
                link(last)
                row_stats(nc, link, stats, mean, var, tmp)
                v.tensor_copy(tmp[:, :], var[:, :]).then_inc(sqrt_in, 1)
                dve.wait_ge(sqrt_done, 1)
                link(v.reciprocal(var[:, :], var[:, :]))

                def normalise(t, b):
                    if not first(t, 2):
                        dve.wait_ge(transposed, t - 1)
                    v.tensor_scalar(normed[b][:, :], x_rows[:, ds(t, 1), :].rearrange("p a c -> p (a c)"),
                                    mean[:, ds(t, 1)], var[:, ds(t, 1)],
                                    ALU.subtract, ALU.mult).then_inc(normed_ready, 1)

                def low(t, b):
                    dve.wait_ge(hi_ready, t + 1)
                    v.tensor_tensor(xlo[b][:, :, :], tp[b][:, 0:C].rearrange("p (k n) -> p k n", k=KC),
                                    xhi[b][:, :, :], ALU.subtract).then_inc(lo_ready, 1)

                normalise(0, 0)
                normalise(1, 1)
                for k in range(KC):
                    for q in range(4):
                        s = slice(q * W4, (q + 1) * W4)
                        dve.wait_ge(w_hi_done, 4 * k + q + 1)
                        v.tensor_tensor(wlo[:, k, s], wst[:, k, s], whi[:, k, s],
                                        ALU.subtract).then_inc(w_lo_done, 1)
                low(0, 0)

                dve.wait_ge(e_loaded, 64)
                v.scalar_tensor_tensor(out=edges["row"][:, :], in0=reli[:, :], scalar=float(NPAD),
                                       in1=srci[:, :], op0=ALU.mult, op1=ALU.add)
                link(v.tensor_copy(edges["dst"][:, :], dsti[:, :]))
                link(v.tensor_reduce(ends[:, 0:NCH], edges["dst"][:, :].rearrange("p (k i) -> p k i", i=EPT),
                                     AX.X, ALU.max))
                link(v.tensor_reduce(ends[:, NCH:2 * NCH], edges["dst"][:, :].rearrange("p (k i) -> p k i", i=EPT),
                                     AX.X, ALU.min))
                v.tensor_scalar(ends[:, NCH:2 * NCH], ends[:, NCH:2 * NCH], -1.0, None,
                                ALU.mult).then_inc(ends_in, 1)

                def body(t, half, b, follow):
                    if follow >= 2:
                        normalise(t + 2, b)
                    if follow >= 1:
                        low(t + 1, 1 - b)
                    for g in (1, 3, 5, 7):
                        dve.wait_ge(group_done, 8 * t + g + 1)
                        if g == 1 and not first(t, 2):
                            dve.wait_ge(stored[b], 16 * half)
                        v.tensor_copy(stage[b][:, g * 512:(g + 1) * 512],
                                      out4[g % 4][:, :]).then_inc(odd_out, 1)
                over_tiles(dve, body)

                dve.wait_ge(ends_out, 1)
                link(v.tensor_scalar(ends_all[:, NCH:2 * NCH], ends_all[:, NCH:2 * NCH], -1.0, None, ALU.mult))
                link(v.tensor_copy(endi[:, :], ends_all[:, :]))
                link(v.tensor_scalar(endi[:, :], endi[:, :], 7, None, ALU.arith_shift_right))
                link(v.tensor_copy(endf[:, :], endi[:, :]))
                hi_t, lo_t = endf[:, 0:NCH], endf[:, NCH:2 * NCH]
                link(v.tensor_tensor(steps[:, :], hi_t, lo_t, ALU.subtract))
                link(v.tensor_scalar(steps[:, :], steps[:, :], 1.0, None, ALU.add))
                link(v.memset(ones_row[:, :], 1.0))
                link(v.tensor_tensor_scan(stepsum[:, :], ones_row[:, :], steps[:, :], 0.0, ALU.mult, ALU.add))
                link(v.tensor_copy(edges["step_end"][:, :], stepsum[:, :]))
                link(v.tensor_tensor(steps[:, :], stepsum[:, :], steps[:, :], ALU.subtract))
                link(v.tensor_copy(edges["step_begin"][:, :], steps[:, :]))
                link(v.tensor_tensor(steps[:, :], lo_t, steps[:, :], ALU.subtract))
                link(v.tensor_copy(edges["tile_of_step"][:, :], steps[:, :]))

            @block.tensor
            def _(pe):
                mm = nc.tensor.matmul

                def turn(t, b):
                    pe.wait_ge(normed_ready, t + 1)
                    if not first(t, 2):
                        pe.wait_ge(lo_ready, t - 1)
                    for k in range(KC):
                        last = nc.tensor.transpose(tp[b][:, k * P:(k + 1) * P], normed[b][:, k * P:(k + 1) * P],
                                                   cst["ident"][:, :])
                    last.then_inc(transposed, 1)

                def body(t, half, b, follow):
                    if follow >= 1:
                        turn(t + 1, 1 - b)
                    pe.wait_ge(lo_ready, t + 1)
                    if first(t):
                        pe.wait_ge(w_lo_done, 4 * KC)
                    for g in range(8):
                        if not (first(t) and g < 4):
                            pe.wait_ge(even_out if g % 2 == 0 else odd_out, 4 * t + g // 2 - 1)
                        s = slice(g * 512, (g + 1) * 512)
                        mm(out4[g % 4][:, :], xhi[b][:, 0, :], whi[:, 0, s], start=True, stop=False)
                        mm(out4[g % 4][:, :], xhi[b][:, 0, :], wlo[:, 0, s], start=False, stop=False)
                        mm(out4[g % 4][:, :], xhi[b][:, 1, :], whi[:, 1, s], start=False, stop=False)
                        mm(out4[g % 4][:, :], xhi[b][:, 1, :], wlo[:, 1, s], start=False, stop=False)
                        mm(out4[g % 4][:, :], xlo[b][:, 0, :], whi[:, 0, s], start=False, stop=False)
                        mm(out4[g % 4][:, :], xlo[b][:, 1, :], whi[:, 1, s], start=False,
                           stop=True).then_inc(group_done, 1)
                turn(0, 0)
                over_tiles(pe, body)


def aggregate(nc, cst, x_rows, edges, table, xs_dram):
    ctx = ExitStack()
    with ctx:
        def sb(name, shape, dt=F32):
            return ctx.enter_context(nc.sbuf_tensor(name, shape, dt))

        def sem(name):
            return ctx.enter_context(nc.semaphore(name))

        rows = [sb(f"gathered{b}", [P, EPT, C]) for b in range(2)]
        index = [sb(f"gather_index{b}", [P, EPT], I32) for b in range(2)]
        token = [sb(f"token{b}", [P, 1]) for b in range(2)]
        pick = sb("pick", [P, EPT, P])
        rel_dst = sb("rel_dst", [P, EPT])
        weight = sb("weight", [P, EPT])
        zeros = sb("zeros", [P, 4 * C])
        acc = ctx.enter_context(nc.psum_tensor("node_sum", [P, 512], F32))

        index_ready = sem("index_ready")
        gathered = [sem(f"rows_gathered{b}") for b in range(2)]
        weight_ready, rel_ready, pick_ready = sem("weight_ready"), sem("rel_ready"), sem("pick_ready")
        step_done, added = sem("step_done"), sem("added")
        zero_ready, zero_stored = sem("zero_ready"), sem("zero_stored")

        def over_chunks(eng, body):
            body(0, 0, 0)
            body(1, 0, 1)
            with eng.Fori(1, NCH // 2) as i:
                body(2 * i, i, 0)
                body(2 * i + 1, i, 1)

        def steps_of(eng, k):
            lo = eng.value_load(edges["step_begin"][0:1, ds(k, 1)], min_val=0, max_val=NCH * NT)
            hi = eng.value_load(edges["step_end"][0:1, ds(k, 1)], min_val=1, max_val=NCH * NT)
            return lo, hi

        with nc.Block() as block:
            @block.sync
            def _(sp):
                sp.wait_ge(zero_ready, 1)
                n = SLOTS // (4 * P)
                for i in range(n):
                    sp.dma_start(xs_dram[i * 4 * P:(i + 1) * 4 * P, :].rearrange("(p a) c -> p (a c)", p=P),
                                 zeros[:, :]).then_inc(zero_stored, 16)
                sp.wait_ge(zero_stored, 16 * n)

            @block.gpsimd
            def _(pool):
                def body(k, half, b):
                    if not (isinstance(k, int) and k < 2):
                        end = pool.value_load(edges["step_end"][0:1, ds(k - 2, 1)], min_val=1, max_val=NCH * NT)
                        pool.wait_ge(step_done, end)
                    nc.gpsimd.tensor_copy(index[b][:, :], edges["row"][:, ds(k * EPT, EPT)]).then_inc(index_ready, 1)
                    pool.wait_ge(index_ready, k + 1)
                    nc.gpsimd.tensor_tensor(token[b][:, :], edges["norm"][:, 0:1], edges["norm"][:, 0:1], ALU.add)
                    for i in range(EPT):
                        nc.gpsimd.indirect_dma_start(
                            rows[b][:, i, :], None, table,
                            bass.IndirectOffsetOnAxis(ap=index[b][:, i:i + 1], axis=0)).then_inc(gathered[b], 16)
                over_chunks(pool, body)

            @block.vector
            def _(dve):
                v = nc.vector
                v.memset(zeros[:, :], 0.0).then_inc(zero_ready, 1)

                def body(k, half, b):
                    v.tensor_copy(weight[:, :], edges["norm"][:, ds(k * EPT, EPT)]).then_inc(weight_ready, 1)
                    dve.wait_ge(weight_ready, k + 1)
                    to_tile = dve.value_load(edges["tile_of_step"][0:1, ds(k, 1)],
                                             min_val=-NCH * NT, max_val=NT)
                    lo, hi = steps_of(dve, k)
                    with dve.Fori(lo, hi) as q:
                        tile = nc.s_assert_within(
                            dve.snap(q + to_tile), 0, NT - 1,
                            skip_runtime_bounds_check_because="dst is a node, so its tile is below NT")
                        v.tensor_scalar(rel_dst[:, :], edges["dst"][:, ds(k * EPT, EPT)],
                                        cst["tile_base"][:, ds(tile, 1)], None,
                                        ALU.subtract).then_inc(rel_ready, 1)
                        dve.wait_ge(rel_ready, q + 1)
                        for i in range(EPT):
                            last = v.tensor_scalar(pick[:, i, :], cst["node_id"][:, :], rel_dst[:, i:i + 1],
                                                   weight[:, i:i + 1], ALU.is_equal, ALU.mult)
                            if i in (0, 3, EPT - 1):
                                last.then_inc(pick_ready, 1)
                        dve.wait_ge(step_done, q + 1)
                        node = x_rows[:, ds(tile, 1), :].rearrange("p a c -> p (a c)")
                        v.tensor_tensor(node, node, acc[:, 0:C], ALU.add).then_inc(added, 1)
                        dve.wait_ge(added, q + 1)
                over_chunks(dve, body)

            @block.tensor
            def _(pe):
                def body(k, half, b):
                    pe.wait_ge(gathered[b], 16 * EPT * (half + 1))
                    lo, hi = steps_of(pe, k)
                    with pe.Fori(lo, hi) as q:
                        for i in range(EPT):
                            if i in (0, 1, 4):
                                pe.wait_ge(pick_ready, 3 * q + (1, 2, None, None, 3)[i])
                            last = nc.tensor.matmul(acc[:, 0:C], pick[:, i, :], rows[b][:, i, :],
                                                    start=(i == 0), stop=(i == EPT - 1))
                        last.then_inc(step_done, 1)
                over_chunks(pe, body)



def route(nc, cst, x_rows, plan, w, x2_dram, xs_dram, router, w13_in, w2_in):
    ctx = ExitStack()
    with ctx:
        def sb(name, shape, dt=F32):
            return ctx.enter_context(nc.sbuf_tensor(name, shape, dt))

        def sem(name):
            return ctx.enter_context(nc.semaphore(name))

        PIECES = [(W_HI13, W_LO13, i * (W13 // 2), W13 // 2) for i in range(2 * KC)] + \
                 [(W_HI2, W_LO2, i * (W2 // 2), W2 // 2) for i in range(2)]
        NP = len(PIECES)
        wst = [sb(f"wf_stage{b}", [P, W2 // 2]) for b in range(2)]
        stats = sb("ln2_stats", [P, NT, 6])
        mean, var, tmp = sb("ln2_mean", [P, NT]), sb("ln2_var", [P, NT]), sb("ln2_tmp", [P, NT])
        turning = sb("h_rows_and_hT", [P, 4, C])
        hrow, hT = [turning[:, b, :] for b in range(2)], [turning[:, 2 + b, :] for b in range(2)]
        rw = sb("router_w", [P, KC, N_EXP])
        lg, tm, s1, s2, l2 = (sb(n, [P, NT, N_EXP]) for n in
                              ("logits", "route_tmp", "choice1", "choice2", "logits2"))
        po = lg
        words = stats[:, :, :].rearrange("p t s -> p (t s)")
        m1, m2, wm, ssum = (words[:, i * NT:(i + 1) * NT] for i in range(4))
        NE = NT * N_EXP
        both = turning[:, 0, 0:NE // 2].bitcast(F16).rearrange("p (t e) -> p t e", e=N_EXP)
        exj = turning[:, 1, 0:NJ]
        cnt, tiles, tiles_in, one8 = (turning[:, 2, i * N_EXP:(i + 1) * N_EXP] for i in range(4))
        cnti = turning[:, 3, 0:N_EXP].bitcast(I32)
        tp = [ctx.enter_context(nc.psum_tensor(f"hT_ps{b}", [P, 512], F32)) for b in range(2)]
        lg_ps = ctx.enter_context(nc.psum_tensor("logits_ps", [P, 512], F32))
        rank_ps = ctx.enter_context(nc.psum_tensor("rank_ps", [P, 512], F32))
        tot_ps = ctx.enter_context(nc.psum_tensor("total_ps", [P, 512], F32))

        spilled, rw_loaded = sem("x2_spilled"), sem("router_loaded")
        chain, sqrt_in, sqrt_done = sem("c_chain"), sem("sqrt2_in"), sem("sqrt2_done")
        normed, transposed, turned, logit_done = (sem(n) for n in
                                                  ("h_normed", "h_transposed", "hT_ready", "logit_done"))
        exp_in, exp_done, both_ready, ranked = (sem(n) for n in ("exp_in", "exp_done", "both_ready", "ranked"))
        kept = sem("rows_kept")
        slots_ready, scattered = sem("slots_ready"), sem("rows_scattered")
        wf_loaded = [sem(f"wf_loaded{b}") for b in range(2)]
        wf_hi, wf_lo = sem("wf_hi"), sem("wf_lo")

        def flat(t):
            return t[:, :, :].rearrange("p t e -> p (t e)")

        def wide(t):
            return t[:, :].unsqueeze(2).to_broadcast([P, NT, N_EXP])

        def over_pieces(eng, body):
            def expert(e):
                for i, (hi, lo, at, n) in enumerate(PIECES):
                    body(NP * e + i, NP // 2 * e + i // 2, i % 2, e, hi, lo, at, n)
            expert(0)
            with eng.Fori(1, N_EXP) as e:
                expert(e)

        def over_tiles(eng, body):
            body(0, 0)
            with eng.Fori(0, NT // 2) as i:
                body(2 * i + 1, 1)
                body(2 * i + 2, 0)

        def early(n, below=2):
            return isinstance(n, int) and n < below

        with nc.Block() as block:
            @block.sync
            def _(sp):
                sp.dma_start(x2_dram, x_rows[:, :, :]).then_inc(spilled, 16)
                sp.dma_start(rw[:, :, :], router).then_inc(rw_loaded, 16)

                def load(n, turn, b, e, hi, lo, at, size):
                    if not early(n):
                        sp.wait_ge(wf_lo, n - 1)
                    of = (w13_in, at) if hi == W_HI13 else (w2_in, at)
                    sp.dma_start(wst[b][:, 0:size],
                                 of[0][:, ds(e, 1), at:at + size].rearrange("p a n -> p (a n)")
                                 ).then_inc(wf_loaded[b], 16)
                over_pieces(sp, load)
                sp.wait_ge(spilled, 16)

            @block.gpsimd
            def _(pool):
                pool.wait_ge(spilled, 16)

                def keep(t, b):
                    pool.wait_ge(normed, t + 1)
                    nc.gpsimd.tensor_copy(x_rows[:, ds(t, 1), :].rearrange("p a c -> p (a c)"),
                                          hrow[b][:, :]).then_inc(kept, 1)
                over_tiles(pool, keep)
                pool.wait_ge(kept, NT)
                pool.wait_ge(slots_ready, 1)
                for t in range(NT):
                    n = P if t < NT - 1 else LAST
                    for slot in plan["slot"]:
                        nc.gpsimd.indirect_dma_start(
                            xs_dram, bass.IndirectOffsetOnAxis(ap=slot[0:n, t:t + 1], axis=0),
                            x_rows[0:n, t, :], None).then_inc(scattered, 16)
                pool.wait_ge(scattered, 32 * NT)

            @block.scalar
            def _(act):
                act.wait_ge(sqrt_in, 1)
                nc.scalar.activation(var[:, :], var[:, :], ACT.Sqrt).then_inc(sqrt_done, 1)

                def copy(t, b):
                    act.wait_ge(transposed, t + 1)
                    if not early(t):
                        act.wait_ge(logit_done, t - 1)
                    nc.scalar.activation(hT[b][:, :], tp[b][:, 0:C], ACT.Copy).then_inc(turned, 1)
                over_tiles(act, copy)
                act.wait_ge(exp_in, 1)
                nc.scalar.activation(flat(l2), flat(l2), ACT.Exp).then_inc(exp_done, 1)
                nc.scalar.activation(m2[:, :], m2[:, :], ACT.Exp).then_inc(exp_done, 1)

                def high(n, turn, b, e, hi, lo, at, size):
                    act.wait_ge(wf_loaded[b], 16 * turn + 16)
                    nc.scalar.activation(w[:, ds(e, 1), hi + at:hi + at + size].rearrange("p a n -> p (a n)"),
                                         wst[b][:, 0:size], ACT.Copy).then_inc(wf_hi, 1)
                over_pieces(act, high)

            @block.vector
            def _(dve):
                v = nc.vector
                link = chained(dve, chain)
                for t in range(NT):
                    last = v.bn_stats(stats[:, t, :], x_rows[:, t, :])
                link(last)
                row_stats(nc, link, stats, mean, var, tmp)
                v.tensor_copy(tmp[:, :], var[:, :]).then_inc(sqrt_in, 1)
                dve.wait_ge(sqrt_done, 1)
                link(v.reciprocal(var[:, :], var[:, :]))

                def normalise(t, b):
                    if not early(t):
                        dve.wait_ge(transposed, t - 1)
                        dve.wait_ge(kept, t - 1)
                    row = x_rows[:, ds(t, 1), :].rearrange("p a c -> p (a c)")
                    v.tensor_scalar(hrow[b][:, :], row, mean[:, ds(t, 1)], var[:, ds(t, 1)],
                                    ALU.subtract, ALU.mult).then_inc(normed, 1)
                over_tiles(dve, normalise)

                def first_of(choice, values, top):
                    link(v.tensor_reduce(top[:, :], values[:, :, :], AX.X, ALU.max))
                    link(v.tensor_tensor(tm[:, :, :], values[:, :, :], wide(top), ALU.is_equal))
                    link(v.tensor_tensor(tm[:, :, :], tm[:, :, :],
                                         cst["first_wins"][:, :].unsqueeze(1).to_broadcast([P, NT, N_EXP]), ALU.mult))
                    link(v.tensor_reduce(wm[:, :], tm[:, :, :], AX.X, ALU.max))
                    link(v.tensor_tensor(choice[:, :, :], tm[:, :, :], wide(wm), ALU.is_equal))

                dve.wait_ge(logit_done, NT)
                dve.wait_ge(kept, NT)
                link(v.tensor_copy(flat(lg), lg_ps[:, 0:NE]))
                first_of(s1, lg, m1)
                link(v.scalar_tensor_tensor(out=flat(l2), in0=flat(s1), scalar=-3e38, in1=flat(lg),
                                            op0=ALU.mult, op1=ALU.add))
                first_of(s2, l2, m2)
                link(v.tensor_tensor(l2[:, :, :], lg[:, :, :], wide(m1), ALU.subtract))
                v.tensor_tensor(m2[:, :], m2[:, :], m1[:, :], ALU.subtract).then_inc(exp_in, 1)
                link(v.tensor_tensor(tm[:, :, :], s1[:, :, :], s2[:, :, :], ALU.add))
                v.tensor_tensor(both[:, :, :], tm[:, :, :],
                                wide(cst["valid"]), ALU.mult).then_inc(both_ready, 1)
                dve.wait_ge(exp_done, 2)
                link(v.tensor_reduce(ssum[:, :], l2[:, :, :], AX.X, ALU.add))
                link(v.reciprocal(ssum[:, :], ssum[:, :]))
                link(v.tensor_tensor(m2[:, :], m2[:, :], ssum[:, :], ALU.mult))
                link(v.tensor_tensor(m1[:, :], m2[:, :], ssum[:, :], ALU.add))
                link(v.tensor_scalar(m1[:, :], m1[:, :], 1e-9, None, ALU.add))
                link(v.reciprocal(m1[:, :], m1[:, :]))
                link(v.tensor_tensor(plan["gate"][0][:, :], ssum[:, :], m1[:, :], ALU.mult))
                link(v.tensor_tensor(plan["gate"][1][:, :], m2[:, :], m1[:, :], ALU.mult))

                def by_expert(t):
                    return flat(t).rearrange("p (e t) -> p e t", e=N_EXP)
                dve.wait_ge(ranked, 2)
                link(v.tensor_copy(by_expert(tm), tot_ps[:, 0:NE].rearrange("p (t e) -> p e t", e=N_EXP)))
                link(v.memset(flat(po), 1.0))
                link(v.memset(by_expert(po)[:, :, 0:1], 0.0))
                link(v.tensor_tensor_scan(flat(l2), flat(po), flat(tm), 0.0, ALU.mult, ALU.add))
                link(v.tensor_copy(cnt[:, :], by_expert(l2)[:, :, NT - 1]))
                link(v.tensor_scalar(cnt[:, :], cnt[:, :], float(TOK - 1), None, ALU.add))
                link(v.tensor_copy(cnti[:, :], cnt[:, :]))
                link(v.tensor_scalar(cnti[:, :], cnti[:, :], TOK.bit_length() - 1, None, ALU.arith_shift_right))
                link(v.tensor_copy(tiles[:, :], cnti[:, :]))
                link(v.memset(one8[:, :], 1.0))
                link(v.tensor_tensor_scan(tiles_in[:, :], one8[:, :], tiles[:, :], 0.0, ALU.mult, ALU.add))
                link(v.tensor_tensor(tiles[:, :], tiles_in[:, :], tiles[:, :], ALU.subtract))
                link(v.tensor_scalar(tiles[:, :], tiles[:, :], float(TOK), None, ALU.mult))
                link(v.tensor_tensor(flat(l2), flat(l2), flat(tm), ALU.subtract))
                link(v.tensor_tensor(by_expert(l2), by_expert(l2),
                                     tiles[:, :].unsqueeze(2).to_broadcast([P, N_EXP, NT]), ALU.add))
                link(v.tensor_tensor(po[:, :, :], rank_ps[:, 0:NE].rearrange("p (t e) -> p t e", e=N_EXP),
                                     by_expert(l2).rearrange("p e t -> p t e"), ALU.add))
                for choice, slot in zip((s1, s2), plan["slot"]):
                    link(v.tensor_tensor(tm[:, :, :], choice[:, :, :], po[:, :, :], ALU.mult))
                    link(v.tensor_reduce(wm[:, :], tm[:, :, :], AX.X, ALU.add))
                    link(v.tensor_copy(slot[:, :], wm[:, :]))
                v.engine_nop().then_inc(slots_ready, 1)
                link(v.tensor_scalar(exj[:, :], cst["slot_tile"][:, :], tiles_in[:, 0:1], None, ALU.is_ge))
                for e in range(1, N_EXP - 1):
                    link(v.scalar_tensor_tensor(out=exj[:, :], in0=cst["slot_tile"][:, :], scalar=tiles_in[:, e:e + 1],
                                                in1=exj[:, :], op0=ALU.is_ge, op1=ALU.add))
                link(v.tensor_scalar(exj[:, :], exj[:, :], float(WPE), None, ALU.mult))
                link(v.tensor_copy(plan["weights_at"][:, :], exj[:, :]))

                def low(n, turn, b, e, hi, lo, at, size):
                    dve.wait_ge(wf_hi, n + 1)
                    v.tensor_tensor(w[:, ds(e, 1), lo + at:lo + at + size].rearrange("p a n -> p (a n)"),
                                    wst[b][:, 0:size],
                                    w[:, ds(e, 1), hi + at:hi + at + size].rearrange("p a n -> p (a n)"),
                                    ALU.subtract).then_inc(wf_lo, 1)
                over_pieces(dve, low)

            @block.tensor
            def _(pe):
                def turn(t, b):
                    pe.wait_ge(normed, t + 1)
                    if not early(t):
                        pe.wait_ge(turned, t - 1)
                    for k in range(KC):
                        last = nc.tensor.transpose(tp[b][:, k * P:(k + 1) * P],
                                                   hrow[b][:, k * P:(k + 1) * P], cst["ident"][:, :])
                    last.then_inc(transposed, 1)

                def logits(t, b):
                    pe.wait_ge(turned, t + 1)
                    for k in range(KC):
                        last = nc.tensor.matmul(lg_ps[:, ds(t * N_EXP, N_EXP)], hT[b][:, k * P:(k + 1) * P],
                                                rw[:, k, :], start=(k == 0), stop=(k == KC - 1))
                    last.then_inc(logit_done, 1)

                pe.wait_ge(rw_loaded, 16)
                turn(0, 0)
                with pe.Fori(0, NT // 2) as i:
                    turn(2 * i + 1, 1)
                    logits(2 * i, 0)
                    turn(2 * i + 2, 0)
                    logits(2 * i + 1, 1)
                logits(NT - 1, 0)
                pe.wait_ge(both_ready, 1)
                nc.tensor.matmul(rank_ps[:, 0:NE], cst["lower"][:, :], flat(both),
                                 start=True, stop=True).then_inc(ranked, 1)
                nc.tensor.matmul(tot_ps[:, 0:NE], cst["ones"][:, :], flat(both),
                                 start=True, stop=True).then_inc(ranked, 1)


def experts(nc, cst, plan, w, room, xs_dram, ys_dram):
    ctx = ExitStack()
    with ctx:
        def sem(name):
            return ctx.enter_context(nc.semaphore(name))

        TT = TOK // P
        taken = [0]

        def sb(name, shape, dt=F32):
            size = 1
            for n in shape[1:]:
                size *= n
            words = size if dt == F32 else size // 2
            part = room[:, taken[0]:taken[0] + words]
            taken[0] += words
            if dt != F32:
                part = part.bitcast(dt)
            if len(shape) == 3:
                part = part.rearrange("p (a b) -> p a b", a=shape[1])
            return part

        xt = [sb(f"slot_rows{b}", [P, TT, C]) for b in range(2)]
        xhi = [sb(f"s_hi{b}", [P, KC, TOK], F16) for b in range(2)]
        xlo = [sb(f"s_lo{b}", [P, KC, TOK], F16) for b in range(2)]
        silu = [sb(f"silu{b}", [P, TOK]) for b in range(2)]
        hid = [sb(f"hidden{b}", [P, TOK]) for b in range(2)]
        hhi = [sb(f"h_hi{b}", [P, NM, TOK], F16) for b in range(2)]
        hlo = [sb(f"h_lo{b}", [P, NM, TOK], F16) for b in range(2)]
        ys = [sb(f"y_rows{b}", [P, TT, C]) for b in range(2)]
        ring = [ctx.enter_context(nc.psum_tensor(f"h13_{b}", [P, 512], F32)) for b in range(4)]
        tp = ctx.enter_context(nc.psum_tensor("slot_T", [P, KC, TOK], F32))
        yp = [ctx.enter_context(nc.psum_tensor(f"y_ps{b}", [P, TT, C], F32)) for b in range(2)]

        loaded = [sem(f"slots_loaded{b}") for b in range(2)]
        stored = [sem(f"y_stored{b}") for b in range(2)]
        turned, xhi_ready, xlo_ready = sem("slots_turned"), sem("slots_hi"), sem("slots_lo")
        grp, silu_ready, mul_done = sem("h13_done"), sem("silu_ready"), sem("mul_done")
        hhi_ready, hlo_ready = sem("h_hi_ready"), sem("h_lo_ready")
        y_done, y_out = sem("y_done"), sem("y_out")

        def over_tiles(eng, body):
            body(0, 0, 0, True)
            body(1, 0, 1, True)
            with eng.Fori(1, NJ // 2 - 1) as i:
                body(2 * i, i, 0, True)
                body(2 * i + 1, i, 1, True)
            body(NJ - 2, NJ // 2 - 1, 0, True)
            body(NJ - 1, NJ // 2 - 1, 1, False)

        def early(n, below=2):
            return isinstance(n, int) and n < below

        def part(m):
            return P if m < HM else 64

        with nc.Block() as block:
            @block.sync
            def _(sp):
                def load(j, half, b):
                    if not early(j):
                        sp.wait_ge(turned, j - 1)
                    sp.dma_start(xt[b][:, :, :], xs_dram[ds(j * TOK, TOK), :].rearrange("(a p) c -> p a c", p=P)
                                 ).then_inc(loaded[b], 16)

                def body(j, half, b, follow):
                    if follow:
                        load(j + 1, half + b, 1 - b)
                    if not early(j):
                        store(j - 2, b)

                def store(j, b):
                    sp.wait_ge(y_out, j + 1)
                    sp.dma_start(ys_dram[ds(j * TOK, TOK), :].rearrange("(a p) c -> p a c", p=P),
                                 ys[b][:, :, :]).then_inc(stored[b], 16)
                load(0, 0, 0)
                over_tiles(sp, body)
                store(NJ - 2, 0)
                store(NJ - 1, 1)
                for b in range(2):
                    sp.wait_ge(stored[b], 16 * (NJ // 2))

            @block.scalar
            def _(act):
                a = nc.scalar.activation

                def x_high(j, half, b):
                    act.wait_ge(turned, j + 1)
                    if not early(j):
                        act.wait_ge(grp, NM * (j - 1))
                    a(xhi[b][:, :, :], tp[:, :, :], ACT.Copy).then_inc(xhi_ready, 1)

                def y_copy(j, half, b):
                    act.wait_ge(y_done, j + 1)
                    if not early(j):
                        act.wait_ge(stored[b], 16 * half)
                    a(ys[b][:, :, :], yp[b][:, :, :], ACT.Copy, scale=1.0 / HSCALE).then_inc(y_out, 1)

                def h_high(j, m, b):
                    act.wait_ge(mul_done, NM * j + m + 1)
                    if m == 0 and not early(j):
                        act.wait_ge(y_done, j - 1)
                    n = part(m)
                    a(hhi[b][0:n, m, :], hid[m % 2][0:n, :], ACT.Copy).then_inc(hhi_ready, 1)

                def body(j, half, b, follow):
                    for m in range(NM):
                        n = part(m)
                        act.wait_ge(grp, NM * j + m + 1)
                        if not (early(j, 1) and m < 2):
                            act.wait_ge(mul_done, NM * j + m - 1)
                        a(silu[m % 2][0:n, :], ring[(NM * b + m) % 4][0:n, 0:TOK], ACT.Silu).then_inc(silu_ready, 1)
                        if m > 0:
                            h_high(j, m - 1, b)
                        if m == 1 and not early(j):
                            y_copy(j - 2, half - 1, b)
                        if m == 3 and follow:
                            x_high(j + 1, half + b, 1 - b)
                    h_high(j, NM - 1, b)
                x_high(0, 0, 0)
                over_tiles(act, body)
                y_copy(NJ - 2, NJ // 2 - 1, 0)
                y_copy(NJ - 1, NJ // 2 - 1, 1)

            @block.vector
            def _(dve):
                v = nc.vector
                def x_low(j, b):
                    dve.wait_ge(xhi_ready, j + 1)
                    v.tensor_tensor(xlo[b][:, :, :], tp[:, :, :], xhi[b][:, :, :], ALU.subtract).then_inc(xlo_ready, 1)

                def h_low(j, m, b):
                    dve.wait_ge(hhi_ready, NM * j + m + 1)
                    n = part(m)
                    v.tensor_tensor(hlo[b][0:n, m, :], hid[m % 2][0:n, :], hhi[b][0:n, m, :],
                                    ALU.subtract).then_inc(hlo_ready, 1)

                def body(j, half, b, follow):
                    for m in range(NM):
                        n = part(m)
                        dve.wait_ge(silu_ready, NM * j + m + 1)
                        if not (early(j, 1) and m < 2):
                            dve.wait_ge(hlo_ready, NM * j + m - 1)
                        bank = ring[(NM * b + m) % 4]
                        h3 = bank[:, TOK:2 * TOK] if m < HM else bank[64:P, 0:TOK]
                        v.scalar_tensor_tensor(out=hid[m % 2][0:n, :], in0=silu[m % 2][0:n, :], scalar=HSCALE,
                                               in1=h3, op0=ALU.mult, op1=ALU.mult).then_inc(mul_done, 1)
                        if m > 0:
                            h_low(j, m - 1, b)
                        if m == 3 and follow:
                            x_low(j + 1, 1 - b)
                    h_low(j, NM - 1, b)
                x_low(0, 0)
                over_tiles(dve, body)

            @block.tensor
            def _(pe):
                mm = nc.tensor.matmul

                def turn(j, half, b):
                    pe.wait_ge(loaded[b], 16 * half + 16)
                    if not early(j, 1):
                        pe.wait_ge(xlo_ready, j)
                    for k in range(KC):
                        for a in range(TT):
                            last = nc.tensor.transpose(tp[:, k, a * P:(a + 1) * P],
                                                       xt[b][:, a, k * P:(k + 1) * P], cst["ident"][:, :])
                    last.then_inc(turned, 1)

                def hidden(j, m, b, at):
                    if not (early(j, 1) and m < 4):
                        pe.wait_ge(mul_done, NM * j + m - 3)
                    for u in range(2 if m < HM else 1):
                        out = ring[(NM * b + m) % 4][:, u * TOK:(u + 1) * TOK]
                        c0 = (2 * m + u) * P
                        n = 0
                        for k in range(KC):
                            hi = w[:, ds(at + (W_HI13 + k * W13 + c0), P)]
                            lo = w[:, ds(at + (W_LO13 + k * W13 + c0), P)]
                            for weights, x in ((hi, xhi), (hi, xlo), (lo, xhi)):
                                last = mm(out, weights, x[b][:, k, :], start=(n == 0), stop=(n == 3 * KC - 1))
                                n += 1
                    last.then_inc(grp, 1)

                def project(j, b, at):
                    pe.wait_ge(hlo_ready, NM * (j + 1))
                    if not early(j):
                        pe.wait_ge(y_out, j - 1)
                    for a in range(TT):
                        n = 0
                        for m in range(NM):
                            r = part(m)
                            hi = w[0:r, ds(at + (W_HI2 + m * C), C)]
                            lo = w[0:r, ds(at + (W_LO2 + m * C), C)]
                            s = slice(a * P, (a + 1) * P)
                            for x, weights in ((hhi, hi), (hhi, lo), (hlo, hi)):
                                last = mm(yp[b][:, a, :], x[b][0:r, m, s], weights, start=(n == 0),
                                          stop=(n == 3 * NM - 1))
                                n += 1
                    last.then_inc(y_done, 1)

                def weights_at(j):
                    return pe.value_load(plan["weights_at"][0:1, ds(j, 1)], min_val=0, max_val=(N_EXP - 1) * WPE)

                def body(j, half, b, follow):
                    at = weights_at(j)
                    pe.wait_ge(xlo_ready, j + 1)
                    for m in range(NM):
                        hidden(j, m, b, at)
                        if m == 2 and follow:
                            turn(j + 1, half + b, 1 - b)
                    if not early(j, 1):
                        project(j - 1, 1 - b, weights_at(j - 1))
                turn(0, 0, 0)
                over_tiles(pe, body)
                project(NJ - 1, 1, weights_at(NJ - 1))


def combine(nc, plan, x2, x2_dram, ys_dram, out):
    ctx = ExitStack()
    with ctx:
        def sb(name, shape, dt=F32):
            return ctx.enter_context(nc.sbuf_tensor(name, shape, dt))

        def sem(name):
            return ctx.enter_context(nc.semaphore(name))

        NB = 4
        y = [[sb(f"y_of{c}_{b}", [P, C]) for b in range(NB)] for c in range(2)]
        x2_loaded = sem("x2_loaded")
        y_loaded = [sem(f"y_loaded{b}") for b in range(NB)]
        chain, mixed, stored = sem("e_chain"), sem("mixed"), sem("out_stored")

        with nc.Block() as block:
            @block.sync
            def _(sp):
                sp.dma_start(x2[:, :, :], x2_dram).then_inc(x2_loaded, 16)
                G = 7
                for g in range(0, NT - 1, G):
                    n = min(G, NT - 1 - g)
                    sp.wait_ge(mixed, g + n)
                    sp.dma_start(out[g * P:(g + n) * P, :].rearrange("(t p) c -> p t c", p=P),
                                 x2[:, g:g + n, :]).then_inc(stored, 16)
                sp.wait_ge(mixed, NT)
                sp.dma_start(out[(NT - 1) * P:N_NODES, :], x2[0:LAST, NT - 1, :]).then_inc(stored, 16)
                sp.wait_ge(stored, 16 * (-(-(NT - 1) // G) + 1))

            @block.gpsimd
            def _(pool):
                for t in range(NT):
                    n, b = (P if t < NT - 1 else LAST), t % NB
                    if t >= NB:
                        pool.wait_ge(mixed, t - NB + 1)
                    for c, slot in enumerate(plan["slot"]):
                        nc.gpsimd.indirect_dma_start(
                            y[c][b][0:n, :], None, ys_dram,
                            bass.IndirectOffsetOnAxis(ap=slot[0:n, t:t + 1], axis=0)).then_inc(y_loaded[b], 16)

            @block.vector
            def _(dve):
                dve.wait_ge(x2_loaded, 16)
                for t in range(NT):
                    n, b = (P if t < NT - 1 else LAST), t % NB
                    dve.wait_ge(y_loaded[b], 32 * (t // NB + 1))
                    for c in range(2):
                        last = nc.vector.scalar_tensor_tensor(
                            out=x2[0:n, t, :], in0=y[c][b][0:n, :], scalar=plan["gate"][c][0:n, t:t + 1],
                            in1=x2[0:n, t, :], op0=ALU.mult, op1=ALU.add)
                        if c == 0:
                            last.then_inc(chain, 1)
                            dve.wait_ge(chain, t + 1)
                    last.then_inc(mixed, 1)


def gnn_then_experts(nc, x, src, dst, rel, norm, gnn_w, router, w13, w2, out):
    table = nc.dram_tensor("rel_table", [N_RELS * NPAD, C], F32).ap()
    x2_dram = nc.dram_tensor("x2_rows", [P, NT, C], F32).ap()
    xs_dram = nc.dram_tensor("slot_inputs", [SLOTS, C], F32).ap()
    ys_dram = nc.dram_tensor("slot_outputs", [SLOTS, C], F32).ap()
    with ExitStack() as ctx:
        def sb(name, shape, dt=F32):
            return ctx.enter_context(nc.sbuf_tensor(name, shape, dt))
        cst = constants(nc, ctx)
        plan = {"slot": [sb(f"slot_of{c}", [P, NT], I32) for c in range(2)],
                "gate": [sb(f"gate_of{c}", [P, NT]) for c in range(2)],
                "weights_at": sb("weights_at", [P, NJ], I32)}
        x_rows = sb("x_rows", [P, NT, C])
        with ExitStack() as edge_ctx:
            def eb(name, shape, dt):
                return edge_ctx.enter_context(nc.sbuf_tensor(name, shape, dt))
            edges = {"row": eb("edge_row", [P, NCH * EPT], I32), "dst": eb("edge_dst", [P, NCH * EPT], F32),
                     "norm": eb("edge_norm", [P, NCH * EPT], F32),
                     "step_begin": eb("step_begin", [P, NCH], I32), "step_end": eb("step_end", [P, NCH], I32),
                     "tile_of_step": eb("tile_of_step", [P, NCH], I32)}
            transform(nc, cst, x_rows, edges, x, gnn_w, src, dst, rel, norm, table)
            aggregate(nc, cst, x_rows, edges, table, xs_dram)
        with nc.sbuf_tensor("expert_w", [P, N_EXP, WPE], F16) as w:
            route(nc, cst, x_rows, plan, w, x2_dram, xs_dram, router, w13, w2)
            experts(nc, cst, plan, w[:, :, :].rearrange("p e n -> p (e n)"),
                    x_rows[:, :, :].rearrange("p t c -> p (t c)"), xs_dram, ys_dram)
        combine(nc, plan, x_rows, x2_dram, ys_dram, out)


def kernel(x, src, dst, edge_type_16, edge_weight1, L0_gnn_weight, L0_ffn_router_w, L0_ffn_w1, L0_ffn_w2,
           L0_ffn_w3):
    import numpy as np
    import concourse.bacc as bacc
    from concourse.bass_utils import run_bass_kernel_spmd

    def edges_by_partition(a, pad):
        flat = np.full(NCH * CHUNK, pad, a.dtype)
        flat[:N_EDGES] = np.asarray(a).reshape(-1)
        return np.ascontiguousarray(flat.reshape(NCH, P, EPT).transpose(1, 0, 2).reshape(P, NCH * EPT))

    x, gnn, router = np.asarray(x), np.asarray(L0_gnn_weight), np.asarray(L0_ffn_router_w)
    w1, w2, w3 = (np.asarray(a) for a in (L0_ffn_w1, L0_ffn_w2, L0_ffn_w3))
    x_pad = np.zeros((NPAD, C), x.dtype)
    x_pad[:N_NODES] = x
    w13 = np.zeros((N_EXP, KC, P, W13), w1.dtype)
    for of, u in ((w1, 0), (w3, 1)):
        t = of.transpose(0, 2, 1).reshape(N_EXP, KC, P, H)
        for m in range(HM):
            w13[..., (2 * m + u) * P:(2 * m + u + 1) * P] = t[..., m * P:(m + 1) * P]
        w13[..., 2 * HM * P + 64 * u:2 * HM * P + 64 * u + HT] = t[..., HM * P:]
    w13 = np.ascontiguousarray(w13.transpose(2, 0, 1, 3).reshape(P, N_EXP, KC * W13))
    w2p = np.zeros((N_EXP, NM * P, C), w2.dtype)
    w2p[:, :H] = w2.transpose(0, 2, 1)
    w2p = np.ascontiguousarray(w2p.reshape(N_EXP, NM, P, C).transpose(2, 0, 1, 3).reshape(P, N_EXP, W2))
    arrays = {
        "x": x_pad,
        "src": edges_by_partition(np.asarray(src), 0),
        "dst": edges_by_partition(np.asarray(dst), N_NODES - 1),
        "rel": edges_by_partition(np.asarray(edge_type_16), 0),
        "norm": edges_by_partition(np.asarray(edge_weight1), 0),
        "gnn_w": np.ascontiguousarray(gnn),
        "router": np.ascontiguousarray(router.T.reshape(KC, P, N_EXP).transpose(1, 0, 2)),
        "w13": w13,
        "w2": w2p,
    }
    nc = bacc.Bacc("TRN2", target_bir_lowering=False, num_devices=1)
    aps = {n: nc.dram_tensor(n, a.shape, mybir.dt.from_np(a.dtype), kind="ExternalInput").ap()
           for n, a in arrays.items()}
    out = nc.dram_tensor("out", (N_NODES, C), F32, kind="ExternalOutput").ap()
    gnn_then_experts(nc, *aps.values(), out)
    r = run_bass_kernel_spmd(nc, [arrays], core_ids=[0])
    return r.results[0]["out"]
```

```python
from contextlib import ExitStack

import concourse.bass as bass
from concourse import mybir

F32 = mybir.dt.float32
F16 = mybir.dt.float16
I32 = mybir.dt.int32
U32 = mybir.dt.uint32
ALU = mybir.AluOpType
ACT = mybir.ActivationFunctionType
AX = mybir.AxisListType
RMAX = bass.bass_isa.ReduceOp.max
ds = bass.ds

P = 128
N_NODES, C = 6250, 256
N_EDGES = 100000
N_RELS = 16
N_EXP, H = 8, 682
KC = C // P
NT = -(-N_NODES // P)
LAST = N_NODES - (NT - 1) * P
NPAD = NT * P
EPS = 1e-5

EPT = 8
CHUNK = EPT * P
NCH = 2 * -(-N_EDGES // (2 * CHUNK))

TOK = 256
NJ = (2 * N_NODES + N_EXP * (TOK - 1)) // TOK
SLOTS = NJ * TOK
HM = H // P
HT = H - HM * P
NM = HM + 1
W13 = (2 * HM + 1) * P
W2 = NM * C
WPE = KC * W13 + W2
W_LOW = N_EXP * WPE
NP = 8 * N_EXP
PIECE = W_LOW // NP
CW = C + 2
HSCALE = 1.0 / 16
assert NJ % 2 == 0 and NT % 2 == 1 and HT <= 64


def chained(eng, sem):
    count = [0]

    def link(ins):
        count[0] += 1
        ins.then_inc(sem, 1)
        eng.wait_ge(sem, count[0])
    return link


def row_stats(nc, link, stats, mean, var, tmp):
    v = nc.vector
    me, m2e, mo, m2o = stats[:, :, 1], stats[:, :, 2], stats[:, :, 4], stats[:, :, 5]
    link(v.tensor_tensor(tmp[:, :], me, mo, ALU.subtract))
    link(v.tensor_tensor(mean[:, :], me, mo, ALU.add))
    link(v.tensor_tensor(var[:, :], m2e, m2o, ALU.add))
    link(v.tensor_tensor(tmp[:, :], tmp[:, :], tmp[:, :], ALU.mult))
    link(v.tensor_scalar(mean[:, :], mean[:, :], 0.5, None, ALU.mult))
    link(v.tensor_scalar(var[:, :], var[:, :], 1.0 / C, EPS, ALU.mult, ALU.add))
    link(v.scalar_tensor_tensor(out=var[:, :], in0=tmp[:, :], scalar=0.25, in1=var[:, :],
                                op0=ALU.mult, op1=ALU.add))


def constants(nc, ctx, edge_ctx):
    def sb(name, shape, dt=F32, ctx=ctx):
        return ctx.enter_context(nc.sbuf_tensor(name, shape, dt))
    c = {
        "ident": sb("ident", [P, P]),
        "lower": sb("lower", [P, P], F16),
        "ones": sb("ones", [P, P], F16),
        "first_wins": sb("first_wins", [P, N_EXP]),
        "slot_tile": sb("slot_tile", [P, NJ]),
        "valid": sb("valid", [P, NT]),
        "node_id": sb("node_id", [P, 2 * P], F16, edge_ctx),
        "tile_base": sb("tile_base", [P, NT + 1], F32, edge_ctx),
        "free_row": sb("free_row", [P, TOK // P], F32, edge_ctx),
    }
    made = ctx.enter_context(nc.semaphore("const_made"))
    cleared = ctx.enter_context(nc.semaphore("const_cleared"))
    with nc.Block() as block:
        @block.gpsimd
        def _(pool):
            g = nc.gpsimd
            g.memset(c["ident"][:, :], 0.0).then_inc(cleared, 1)
            g.memset(c["lower"][:, :], 0.0).then_inc(cleared, 1)
            g.memset(c["valid"][:, :], 1.0).then_inc(cleared, 1)
            g.memset(c["ones"][:, :], 1.0).then_inc(made, 1)
            opts = dict(channel_multiplier=0, allow_small_or_imprecise_dtypes=True)
            g.iota(c["node_id"][:, :], pattern=[[1, 2 * P]], base=0, **opts).then_inc(made, 1)
            g.iota(c["tile_base"][:, :], pattern=[[P, NT + 1]], base=0, **opts).then_inc(made, 1)
            g.iota(c["first_wins"][:, :], pattern=[[-1, N_EXP]], base=N_EXP, **opts).then_inc(made, 1)
            g.iota(c["slot_tile"][:, :], pattern=[[1, NJ]], base=0, **opts).then_inc(made, 1)
            g.iota(c["free_row"][:, :], pattern=[[P, TOK // P]], base=NPAD, channel_multiplier=1,
                   allow_small_or_imprecise_dtypes=True).then_inc(made, 1)
            pool.wait_ge(cleared, 3)
            g.affine_select(out=c["ident"][:, :], in_=c["ident"][:, :], compare_op=ALU.not_equal,
                            fill=1.0, base=0, pattern=[[-1, P]], channel_multiplier=1).then_inc(made, 1)
            g.affine_select(out=c["lower"][:, :], in_=c["lower"][:, :], compare_op=ALU.is_ge,
                            fill=1.0, base=0, pattern=[[-1, P]], channel_multiplier=1).then_inc(made, 1)
            g.affine_select(out=c["valid"][:, :], in_=c["valid"][:, :], compare_op=ALU.is_ge,
                            fill=0.0, base=N_NODES - 1, pattern=[[-P, NT]],
                            channel_multiplier=-1).then_inc(made, 1)
            pool.wait_ge(made, 9)
    return c


def transform(nc, cst, x_rows, edges, x_in, gw, src, dst, rel, norm, table):
    ctx = ExitStack()
    with ctx:
        def sb(name, shape, dt=F32):
            return ctx.enter_context(nc.sbuf_tensor(name, shape, dt))

        def sem(name):
            return ctx.enter_context(nc.semaphore(name))

        wst = sb("w_stage", [P, KC, N_RELS * C])
        whi = sb("w_hi", [P, KC, N_RELS * C], F16)
        wlo = sb("w_lo", [P, KC, N_RELS * C], F16)
        stage = [sb(f"row_stage{b}", [P, N_RELS * C]) for b in range(2)]
        normed = [sb(f"normed{b}", [P, C]) for b in range(2)]
        xhi = [sb(f"x_hi{b}", [P, KC, P], F16) for b in range(2)]
        xlo = [sb(f"x_lo{b}", [P, KC, P], F16) for b in range(2)]
        stats = sb("ln_stats", [P, NT, 6])
        mean, var, tmp = sb("ln_mean", [P, NT]), sb("ln_var", [P, NT]), sb("ln_tmp", [P, NT])
        srci = sb("src_i", [P, NCH * EPT], I32)
        reli = sb("rel_i", [P, NCH * EPT], I32)
        dsti = sb("dst_i", [P, NCH * EPT], I32)
        ends = sb("chunk_ends", [P, 2 * NCH])
        ends_all = sb("chunk_ends_all", [P, 2 * NCH])
        endi = sb("chunk_ends_i", [P, 2 * NCH], I32)
        endf = sb("chunk_ends_f", [P, 2 * NCH])
        steps = sb("chunk_steps", [P, NCH])
        ones_row = sb("ones_row", [P, NCH])
        stepsum = sb("chunk_stepsum", [P, NCH])
        tp = [ctx.enter_context(nc.psum_tensor(f"xT{b}", [P, 512], F32)) for b in range(2)]
        out4 = [ctx.enter_context(nc.psum_tensor(f"rel_out{b}", [P, 512], F32)) for b in range(4)]

        x_loaded = [sem(f"x_loaded{g}") for g in range(7)]
        w_loaded = [sem(f"w_loaded{k}") for k in range(KC)]
        e_loaded = sem("edges_loaded")
        w_hi_done, w_lo_done = sem("w_hi_done"), sem("w_lo_done")
        chain, sqrt_in, sqrt_done = sem("a_chain"), sem("sqrt_in"), sem("sqrt_done")
        normed_ready, transposed = sem("normed_ready"), sem("x_transposed")
        hi_ready, lo_ready = sem("x_hi_ready"), sem("x_lo_ready")
        group_done, even_out, odd_out = sem("group_done"), sem("even_out"), sem("odd_out")
        stored = [sem(f"rows_stored{b}") for b in range(2)]
        ends_in, ends_out = sem("chunk_ends_in"), sem("chunk_ends_out")

        x_v = x_in.rearrange("(t p) c -> p t c", p=P)
        gw_v = gw.rearrange("r (k p) o -> k p r o", p=P)
        table_v = table.rearrange("(r t p) c -> t p r c", r=N_RELS, p=P)
        TG = NT // 7
        W4 = N_RELS * C // 4

        def over_tiles(eng, body):
            body(0, 0, 0, 2)
            with eng.Fori(0, (NT - 3) // 2) as i:
                body(2 * i + 1, i, 1, 2)
                body(2 * i + 2, i + 1, 0, 2)
            body(NT - 2, (NT - 2) // 2, (NT - 2) % 2, 1)
            body(NT - 1, (NT - 1) // 2, (NT - 1) % 2, 0)

        def first(t, n=1):
            return isinstance(t, int) and t < n

        with nc.Block() as block:
            @block.sync
            def _(sp):
                for k in range(KC):
                    sp.dma_start(wst[:, k, :].rearrange("p (r o) -> p r o", r=N_RELS),
                                 gw_v[k]).then_inc(w_loaded[k], 16)

                def body(t, half, b, follow):
                    sp.wait_ge(even_out, 4 * t + 4)
                    sp.wait_ge(odd_out, 4 * t + 4)
                    sp.dma_start(table_v[ds(t, 1)].rearrange("a p r c -> p (a r) c"),
                                 stage[b][:, :].rearrange("p (r c) -> p r c", r=N_RELS)).then_inc(stored[b], 16)
                over_tiles(sp, body)
                sp.wait_ge(stored[0], 16 * ((NT + 1) // 2))
                sp.wait_ge(stored[1], 16 * (NT // 2))

            @block.gpsimd
            def _(pool):
                pool.wait_ge(ends_in, 1)
                nc.gpsimd.partition_all_reduce(ends_all[:, :], ends[:, :], P, RMAX).then_inc(ends_out, 1)
                pool.wait_ge(ends_out, 1)

            @block.scalar
            def _(act):
                for g in range(7):
                    act.dma_start(x_rows[:, g * TG:(g + 1) * TG, :],
                                  x_v[:, g * TG:(g + 1) * TG, :]).then_inc(x_loaded[g], 16)
                for to, of in ((srci, src), (reli, rel), (dsti, dst), (edges["norm"], norm)):
                    act.dma_start(to[:, :], of).then_inc(e_loaded, 16)
                for k in range(KC):
                    act.wait_ge(w_loaded[k], 16)
                    for q in range(4):
                        s = slice(q * W4, (q + 1) * W4)
                        nc.scalar.activation(whi[:, k, s], wst[:, k, s], ACT.Copy).then_inc(w_hi_done, 1)
                act.wait_ge(sqrt_in, 1)
                nc.scalar.activation(var[:, :], var[:, :], ACT.Sqrt).then_inc(sqrt_done, 1)

                def high(t, b):
                    act.wait_ge(transposed, t + 1)
                    if not first(t, 2):
                        act.wait_ge(group_done, 8 * t - 8)
                    nc.scalar.activation(xhi[b][:, :, :], tp[b][:, 0:C].rearrange("p (k n) -> p k n", k=KC),
                                         ACT.Copy).then_inc(hi_ready, 1)

                def body(t, half, b, follow):
                    if follow >= 1:
                        high(t + 1, 1 - b)
                    for g in (0, 2, 4, 6):
                        act.wait_ge(group_done, 8 * t + g + 1)
                        if g == 0 and not first(t, 2):
                            act.wait_ge(stored[b], 16 * half)
                        nc.scalar.activation(stage[b][:, g * 512:(g + 1) * 512], out4[g % 4][:, :],
                                             ACT.Copy).then_inc(even_out, 1)
                high(0, 0)
                over_tiles(act, body)

            @block.vector
            def _(dve):
                v = nc.vector
                link = chained(dve, chain)
                for g in range(7):
                    dve.wait_ge(x_loaded[g], 16)
                    for t in range(g * TG, (g + 1) * TG):
                        last = v.bn_stats(stats[:, t, :], x_rows[:, t, :])
                link(last)
                row_stats(nc, link, stats, mean, var, tmp)
                v.tensor_copy(tmp[:, :], var[:, :]).then_inc(sqrt_in, 1)
                dve.wait_ge(sqrt_done, 1)
                link(v.reciprocal(var[:, :], var[:, :]))

                def normalise(t, b):
                    if not first(t, 2):
                        dve.wait_ge(transposed, t - 1)
                    v.tensor_scalar(normed[b][:, :], x_rows[:, ds(t, 1), :].rearrange("p a c -> p (a c)"),
                                    mean[:, ds(t, 1)], var[:, ds(t, 1)],
                                    ALU.subtract, ALU.mult).then_inc(normed_ready, 1)

                def low(t, b):
                    dve.wait_ge(hi_ready, t + 1)
                    v.tensor_tensor(xlo[b][:, :, :], tp[b][:, 0:C].rearrange("p (k n) -> p k n", k=KC),
                                    xhi[b][:, :, :], ALU.subtract).then_inc(lo_ready, 1)

                normalise(0, 0)
                normalise(1, 1)
                for k in range(KC):
                    for q in range(4):
                        s = slice(q * W4, (q + 1) * W4)
                        dve.wait_ge(w_hi_done, 4 * k + q + 1)
                        v.tensor_tensor(wlo[:, k, s], wst[:, k, s], whi[:, k, s],
                                        ALU.subtract).then_inc(w_lo_done, 1)
                low(0, 0)

                dve.wait_ge(e_loaded, 64)
                v.scalar_tensor_tensor(out=edges["row"][:, :], in0=reli[:, :], scalar=float(NPAD),
                                       in1=srci[:, :], op0=ALU.mult, op1=ALU.add)
                link(v.tensor_copy(edges["dst"][:, :], dsti[:, :]))
                link(v.tensor_reduce(ends[:, 0:NCH], edges["dst"][:, :].rearrange("p (k i) -> p k i", i=EPT),
                                     AX.X, ALU.max))
                link(v.tensor_reduce(ends[:, NCH:2 * NCH], edges["dst"][:, :].rearrange("p (k i) -> p k i", i=EPT),
                                     AX.X, ALU.min))
                v.tensor_scalar(ends[:, NCH:2 * NCH], ends[:, NCH:2 * NCH], -1.0, None,
                                ALU.mult).then_inc(ends_in, 1)

                def body(t, half, b, follow):
                    if follow >= 2:
                        normalise(t + 2, b)
                    if follow >= 1:
                        low(t + 1, 1 - b)
                    for g in (1, 3, 5, 7):
                        dve.wait_ge(group_done, 8 * t + g + 1)
                        if g == 1 and not first(t, 2):
                            dve.wait_ge(stored[b], 16 * half)
                        v.tensor_copy(stage[b][:, g * 512:(g + 1) * 512],
                                      out4[g % 4][:, :]).then_inc(odd_out, 1)
                over_tiles(dve, body)

                dve.wait_ge(ends_out, 1)
                link(v.tensor_scalar(ends_all[:, NCH:2 * NCH], ends_all[:, NCH:2 * NCH], -1.0, None, ALU.mult))
                link(v.tensor_copy(endi[:, :], ends_all[:, :]))
                link(v.tensor_scalar(endi[:, :], endi[:, :], 7, None, ALU.arith_shift_right))
                link(v.tensor_copy(endf[:, :], endi[:, :]))
                hi_t, lo_t = endf[:, 0:NCH], endf[:, NCH:2 * NCH]
                link(v.tensor_scalar(lo_t, lo_t, float(NT - 2), None, ALU.min))
                link(v.tensor_copy(edges["window"][:, :], lo_t))
                link(v.tensor_scalar(ends[:, 0:NCH], lo_t, float(P), None, ALU.mult))
                meta = edges["meta"][:, :].rearrange("p (k m i) -> p k m i", m=2, i=EPT)
                link(v.tensor_tensor(meta[:, :, 0, :], edges["dst"][:, :].rearrange("p (k i) -> p k i", i=EPT),
                                     ends[:, 0:NCH].unsqueeze(2).to_broadcast([P, NCH, EPT]), ALU.subtract))
                link(v.tensor_copy(meta[:, :, 1, :], edges["norm"][:, :].rearrange("p (k i) -> p k i", i=EPT)))
                link(v.tensor_tensor(steps[:, :], hi_t, lo_t, ALU.subtract))
                link(v.tensor_scalar(steps[:, :], steps[:, :], -1.0, 0.0, ALU.add, ALU.max))
                link(v.tensor_reduce(ends[:, 0:1], steps[:, :], AX.X, ALU.add))
                link(v.tensor_copy(edges["steps_past"][:, :], ends[:, 0:1]))
                link(v.tensor_scalar(steps[:, :], steps[:, :], 1.0, None, ALU.add))
                link(v.memset(ones_row[:, :], 1.0))
                link(v.tensor_tensor_scan(stepsum[:, :], ones_row[:, :], steps[:, :], 0.0, ALU.mult, ALU.add))
                link(v.tensor_copy(edges["step_end"][:, :], stepsum[:, :]))
                link(v.tensor_tensor(steps[:, :], stepsum[:, :], steps[:, :], ALU.subtract))
                link(v.tensor_copy(edges["step_begin"][:, :], steps[:, :]))
                link(v.tensor_tensor(steps[:, :], lo_t, steps[:, :], ALU.subtract))
                link(v.tensor_scalar(steps[:, :], steps[:, :], 2.0, None, ALU.add))
                link(v.tensor_copy(edges["tile_of_step"][:, :], steps[:, :]))

            @block.tensor
            def _(pe):
                mm = nc.tensor.matmul

                def turn(t, b):
                    pe.wait_ge(normed_ready, t + 1)
                    if not first(t, 2):
                        pe.wait_ge(lo_ready, t - 1)
                    for k in range(KC):
                        last = nc.tensor.transpose(tp[b][:, k * P:(k + 1) * P], normed[b][:, k * P:(k + 1) * P],
                                                   cst["ident"][:, :])
                    last.then_inc(transposed, 1)

                def body(t, half, b, follow):
                    if follow >= 1:
                        turn(t + 1, 1 - b)
                    pe.wait_ge(lo_ready, t + 1)
                    if first(t):
                        pe.wait_ge(w_lo_done, 4 * KC)
                    for g in range(8):
                        if not (first(t) and g < 4):
                            pe.wait_ge(even_out if g % 2 == 0 else odd_out, 4 * t + g // 2 - 1)
                        s = slice(g * 512, (g + 1) * 512)
                        mm(out4[g % 4][:, :], xhi[b][:, 0, :], whi[:, 0, s], start=True, stop=False)
                        mm(out4[g % 4][:, :], xhi[b][:, 0, :], wlo[:, 0, s], start=False, stop=False)
                        mm(out4[g % 4][:, :], xhi[b][:, 1, :], whi[:, 1, s], start=False, stop=False)
                        mm(out4[g % 4][:, :], xhi[b][:, 1, :], wlo[:, 1, s], start=False, stop=False)
                        mm(out4[g % 4][:, :], xlo[b][:, 0, :], whi[:, 0, s], start=False, stop=False)
                        mm(out4[g % 4][:, :], xlo[b][:, 1, :], whi[:, 1, s], start=False,
                           stop=True).then_inc(group_done, 1)
                turn(0, 0)
                over_tiles(pe, body)


def over_chunks(eng, body, peel=True):
    if peel:
        body(0, 0, 0)
        body(1, 0, 1)
    with eng.Fori(1 if peel else 0, NCH // 2) as i:
        body(2 * i, i, 0)
        body(2 * i + 1, i, 1)


def aggregate(nc, cst, x_rows, edges, table, xs_dram):
    ctx = ExitStack()
    with ctx:
        def sb(name, shape, dt=F32):
            return ctx.enter_context(nc.sbuf_tensor(name, shape, dt))

        def sem(name):
            return ctx.enter_context(nc.semaphore(name))

        rows = [sb(f"gathered{b}", [P, EPT, C]) for b in range(2)]
        high = [sb(f"msg_hi{b}", [P, EPT, C], F16) for b in range(2)]
        low = [sb(f"msg_lo{b}", [P, EPT, C], F16) for b in range(2)]
        pick = [sb(f"pick{b}", [P, EPT, 2 * P], F16) for b in range(2)]
        meta = [sb(f"meta{b}", [P, 2, EPT]) for b in range(2)]
        index = [sb(f"gather_index{b}", [P, 2 * EPT], I32) for b in range(2)]
        token = [sb(f"token{b}", [P, 1]) for b in range(2)]
        free_slots = sb("free_slots", [P, TOK // P, CW])
        acc = [ctx.enter_context(nc.psum_tensor(f"window_sum{b}", [P, 2, 512], F32)) for b in range(2)]

        index_ready, meta_ready = sem("index_ready"), sem("meta_ready")
        gathered = [sem(f"rows_gathered{b}") for b in range(2)]
        high_ready, split_done, summed, added = sem("msg_hi_ready"), sem("msg_split"), sem("summed"), sem("added")
        zero_ready, zero_stored = sem("zero_ready"), sem("zero_stored")

        def early(k):
            return isinstance(k, int) and k < 2

        with nc.Block() as block:
            @block.sync
            def _(sp):
                sp.wait_ge(zero_ready, 2)
                for j in range(NJ):
                    sp.dma_start(xs_dram[j * TOK:(j + 1) * TOK, :].rearrange("(a p) c -> p a c", p=P),
                                 free_slots[:, :, :]).then_inc(zero_stored, 16)
                sp.wait_ge(zero_stored, 16 * NJ)

            @block.gpsimd
            def _(pool):
                def pair(h, into):
                    for b in range(2):
                        if not early(2 * h + b):
                            pool.wait_ge(split_done, 2 * h + b - 1)
                        if b == 0:
                            nc.gpsimd.tensor_copy(index[into][:, :], edges["row"][:, ds(h * 2 * EPT, 2 * EPT)]
                                                  ).then_inc(index_ready, 1)
                            pool.wait_ge(index_ready, h + 1)
                        nc.gpsimd.tensor_tensor(token[b][:, :], edges["norm"][:, 0:1], edges["norm"][:, 0:1],
                                                ALU.add)
                        for i in range(EPT):
                            at = index[into][:, b * EPT + i:b * EPT + i + 1]
                            nc.gpsimd.indirect_dma_start(
                                rows[b][:, i, :], None, table,
                                bass.IndirectOffsetOnAxis(ap=at, axis=0)).then_inc(gathered[b], 16)
                pair(0, 0)
                with pool.Fori(0, (NCH // 2 - 1) // 2) as i:
                    pair(2 * i + 1, 1)
                    pair(2 * i + 2, 0)

            @block.scalar
            def _(act):
                def body(k, half, b):
                    act.wait_ge(meta_ready, k + 1)
                    act.wait_ge(gathered[b], 16 * EPT * (half + 1))
                    if not early(k):
                        act.wait_ge(summed, k - 1)
                    for i in range(EPT):
                        nc.scalar.activation(high[b][:, i, :], rows[b][:, i, :], ACT.Copy,
                                             scale=meta[b][:, 1, i:i + 1]).then_inc(high_ready, 1)
                over_chunks(act, body)

            @block.vector
            def _(dve):
                v = nc.vector
                v.memset(free_slots[:, :, :], 0.0).then_inc(zero_ready, 1)
                dve.wait_ge(zero_ready, 1)
                v.tensor_copy(free_slots[:, :, C], cst["free_row"][:, :]).then_inc(zero_ready, 1)
                v.memset(x_rows[:, NT, :], 0.0).then_inc(zero_ready, 1)

                def add(k, b):
                    at = dve.value_load(edges["window"][0:1, ds(k, 1)], min_val=0, max_val=NT - 2)
                    dve.wait_ge(summed, k + 1)
                    if not (isinstance(k, int) and k < 1):
                        dve.wait_ge(added, k)
                    node = x_rows[:, ds(at, 2), :]
                    v.tensor_tensor(node, node, acc[b][:, :, 0:C], ALU.add).then_inc(added, 1)

                def body(k, half, b):
                    if not early(k):
                        dve.wait_ge(split_done, k - 1)
                        dve.wait_ge(high_ready, EPT * (k - 1))
                    v.tensor_copy(meta[b][:, :, :].rearrange("p m i -> p (m i)"),
                                  edges["meta"][:, ds(k * 2 * EPT, 2 * EPT)]).then_inc(meta_ready, 1)
                    dve.wait_ge(meta_ready, k + 1)
                    if not early(k):
                        dve.wait_ge(summed, k - 1)
                    for i in range(EPT):
                        v.tensor_scalar(pick[b][:, i, :], cst["node_id"][:, :], meta[b][:, 0, i:i + 1],
                                        None, ALU.is_equal)
                    for i in range(EPT):
                        dve.wait_ge(high_ready, EPT * k + i + 1)
                        last = v.scalar_tensor_tensor(out=low[b][:, i, :], in0=rows[b][:, i, :],
                                                      scalar=meta[b][:, 1, i:i + 1], in1=high[b][:, i, :],
                                                      op0=ALU.mult, op1=ALU.subtract)
                    last.then_inc(split_done, 1)
                    if not (isinstance(k, int) and k < 1):
                        add(k - 1, 1 - b)
                over_chunks(dve, body)
                add(NCH - 1, 1)
                dve.wait_ge(zero_ready, 3)

            @block.tensor
            def _(pe):
                def body(k, half, b):
                    pe.wait_ge(split_done, k + 1)
                    if not early(k):
                        pe.wait_ge(added, k - 1)
                    for i in range(EPT):
                        for tile in range(2):
                            for part in (high, low):
                                last = nc.tensor.matmul(
                                    acc[b][:, tile, 0:C], pick[b][:, i, tile * P:(tile + 1) * P], part[b][:, i, :],
                                    start=(i == 0 and part is high), stop=(i == EPT - 1 and part is low))
                    last.then_inc(summed, 1)
                over_chunks(pe, body)


def aggregate_past(nc, cst, x_rows, edges, table):
    ctx = ExitStack()
    with ctx:
        def sb(name, shape, dt=F32):
            return ctx.enter_context(nc.sbuf_tensor(name, shape, dt))

        def sem(name):
            return ctx.enter_context(nc.semaphore(name))

        rows = [sb(f"past_rows{b}", [P, EPT, C]) for b in range(2)]
        index = [sb(f"past_index{b}", [P, EPT], I32) for b in range(2)]
        token = [sb(f"past_token{b}", [P, 1]) for b in range(2)]
        pick = sb("past_pick", [P, EPT, P])
        rel_dst = sb("past_rel_dst", [P, EPT])
        weight = sb("past_weight", [P, EPT])
        acc = ctx.enter_context(nc.psum_tensor("node_sum", [P, 512], F32))
        index_ready = sem("past_index_ready")
        gathered = [sem(f"past_gathered{b}") for b in range(2)]
        weight_ready, rel_ready, pick_ready = sem("past_weight"), sem("past_rel"), sem("past_pick_ready")
        step_done, added = sem("past_step_done"), sem("past_added")

        def steps_of(eng, k):
            lo = eng.value_load(edges["step_begin"][0:1, ds(k, 1)], min_val=0, max_val=NCH * NT)
            hi = eng.value_load(edges["step_end"][0:1, ds(k, 1)], min_val=1, max_val=NCH * NT)
            return lo, hi

        def any_past(eng):
            return eng.value_load(edges["steps_past"][0:1, 0:1], min_val=0, max_val=NCH * NT) > 0

        with nc.Block() as block:
            @block.gpsimd
            def _(pool):
                def body(k, half, b):
                    if not (isinstance(k, int) and k < 2):
                        end = pool.value_load(edges["step_end"][0:1, ds(k - 2, 1)], min_val=1, max_val=NCH * NT)
                        pool.wait_ge(step_done, end)
                    nc.gpsimd.tensor_copy(index[b][:, :], edges["row"][:, ds(k * EPT, EPT)]).then_inc(index_ready, 1)
                    pool.wait_ge(index_ready, k + 1)
                    nc.gpsimd.tensor_tensor(token[b][:, :], edges["norm"][:, 0:1], edges["norm"][:, 0:1], ALU.add)
                    for i in range(EPT):
                        nc.gpsimd.indirect_dma_start(
                            rows[b][:, i, :], None, table,
                            bass.IndirectOffsetOnAxis(ap=index[b][:, i:i + 1], axis=0)).then_inc(gathered[b], 16)
                with pool.If(any_past(pool)):
                    over_chunks(pool, body)

            @block.vector
            def _(dve):
                v = nc.vector

                def body(k, half, b):
                    v.tensor_copy(weight[:, :], edges["norm"][:, ds(k * EPT, EPT)]).then_inc(weight_ready, 1)
                    dve.wait_ge(weight_ready, k + 1)
                    to_tile = dve.value_load(edges["tile_of_step"][0:1, ds(k, 1)],
                                             min_val=-NCH * NT, max_val=NT)
                    lo, hi = steps_of(dve, k)
                    with dve.Fori(lo, hi) as q:
                        tile = nc.s_assert_within(
                            dve.snap(q + to_tile), 0, NT,
                            skip_runtime_bounds_check_because="dst is a node, so its tile is below NT")
                        v.tensor_scalar(rel_dst[:, :], edges["dst"][:, ds(k * EPT, EPT)],
                                        cst["tile_base"][:, ds(tile, 1)], None,
                                        ALU.subtract).then_inc(rel_ready, 1)
                        dve.wait_ge(rel_ready, q + 1)
                        for i in range(EPT):
                            last = v.tensor_scalar(pick[:, i, :], cst["node_id"][:, 0:P], rel_dst[:, i:i + 1],
                                                   weight[:, i:i + 1], ALU.is_equal, ALU.mult)
                        last.then_inc(pick_ready, 1)
                        dve.wait_ge(step_done, q + 1)
                        node = x_rows[:, ds(tile, 1), :].rearrange("p a c -> p (a c)")
                        v.tensor_tensor(node, node, acc[:, 0:C], ALU.add).then_inc(added, 1)
                        dve.wait_ge(added, q + 1)
                with dve.If(any_past(dve)):
                    over_chunks(dve, body)

            @block.tensor
            def _(pe):
                def body(k, half, b):
                    pe.wait_ge(gathered[b], 16 * EPT * (half + 1))
                    lo, hi = steps_of(pe, k)
                    with pe.Fori(lo, hi) as q:
                        pe.wait_ge(pick_ready, q + 1)
                        for i in range(EPT):
                            last = nc.tensor.matmul(acc[:, 0:C], pick[:, i, :], rows[b][:, i, :],
                                                    start=(i == 0), stop=(i == EPT - 1))
                        last.then_inc(step_done, 1)
                with pe.If(any_past(pe)):
                    over_chunks(pe, body)


def route(nc, cst, all_rows, plan, w, out, xs_dram, router, w_in):
    ctx = ExitStack()
    with ctx:
        def sb(name, shape, dt=F32):
            return ctx.enter_context(nc.sbuf_tensor(name, shape, dt))

        def sem(name):
            return ctx.enter_context(nc.semaphore(name))

        x_rows, spare = all_rows[:, 0:NT, 0:C], all_rows[:, NT, 0:C]
        wst = [sb(f"wf_stage{b}", [P, PIECE]) for b in range(3)]
        stats = sb("ln2_stats", [P, NT, 6])
        mean, var, tmp = sb("ln2_mean", [P, NT]), sb("ln2_var", [P, NT]), sb("ln2_tmp", [P, NT])
        turning = sb("h_rows_and_hT", [P, 3, C])
        hrow, hT = [turning[:, b, :] for b in range(2)], [turning[:, 2, :], spare]
        rw = sb("router_w", [P, KC, N_EXP])
        lg, tm, s1, s2, l2 = (sb(n, [P, NT, N_EXP]) for n in
                              ("logits", "route_tmp", "choice1", "choice2", "logits2"))
        po = lg
        words = stats[:, :, :].rearrange("p t s -> p (t s)")
        m1, m2, wm, ssum = (words[:, i * NT:(i + 1) * NT] for i in range(4))
        NE = NT * N_EXP
        both = turning[:, 0, 0:NE // 2].bitcast(F16).rearrange("p (t e) -> p t e", e=N_EXP)
        exj = turning[:, 1, 0:NJ]
        gate2 = turning[:, 1, NJ:NJ + NT]
        cnt, tiles, tiles_in, one8 = (turning[:, 2, i * N_EXP:(i + 1) * N_EXP] for i in range(4))
        cnti = spare[:, 0:N_EXP].bitcast(I32)
        tp = [ctx.enter_context(nc.psum_tensor(f"hT_ps{b}", [P, 512], F32)) for b in range(2)]
        lg_ps = ctx.enter_context(nc.psum_tensor("logits_ps", [P, 512], F32))
        rank_ps = ctx.enter_context(nc.psum_tensor("rank_ps", [P, 512], F32))
        tot_ps = ctx.enter_context(nc.psum_tensor("total_ps", [P, 512], F32))

        spilled, rw_loaded = sem("x2_spilled"), sem("router_loaded")
        chain, sqrt_in, sqrt_done = sem("c_chain"), sem("sqrt2_in"), sem("sqrt2_done")
        normed, transposed, turned, logit_done = (sem(n) for n in
                                                  ("h_normed", "h_transposed", "hT_ready", "logit_done"))
        exp_in, exp_done, both_ready, ranked = (sem(n) for n in ("exp_in", "exp_done", "both_ready", "ranked"))
        kept, noded = sem("rows_kept"), sem("nodes_set")
        slots_ready, scattered = sem("slots_ready"), sem("rows_scattered")
        wf_loaded = [sem(f"wf_loaded{b}") for b in range(3)]
        wf_hi, wf_lo = sem("wf_hi"), sem("wf_lo")

        def flat(t):
            return t[:, :, :].rearrange("p t e -> p (t e)")

        def wide(t):
            return t[:, :].unsqueeze(2).to_broadcast([P, NT, N_EXP])

        def over_pieces(eng, body):
            for n in range(3):
                body(n, 0, n)
            with eng.Fori(1, NP // 3) as i:
                for b in range(3):
                    body(3 * i + b, i, b)
            for n in range(NP // 3 * 3, NP):
                body(n, n // 3, n % 3)

        def over_tiles(eng, body):
            body(0, 0)
            with eng.Fori(0, NT // 2) as i:
                body(2 * i + 1, 1)
                body(2 * i + 2, 0)

        def early(n, below=2):
            return isinstance(n, int) and n < below

        with nc.Block() as block:
            @block.sync
            def _(sp):
                sp.dma_start(out[0:NPAD, :].rearrange("(t p) c -> p t c", p=P), x_rows).then_inc(spilled, 16)
                for a in range(TOK // P):
                    sp.dma_start(out[NPAD + a * P:NPAD + (a + 1) * P, :], spare).then_inc(spilled, 16)
                sp.dma_start(rw[:, :, :], router).then_inc(rw_loaded, 16)

                def load(n, turn, b):
                    if not early(n, 3):
                        sp.wait_ge(wf_lo, n - 2)
                    sp.dma_start(wst[b][:, :], w_in[:, ds(n * PIECE, PIECE)]).then_inc(wf_loaded[b], 16)
                over_pieces(sp, load)
                sp.wait_ge(spilled, 48)

            @block.gpsimd
            def _(pool):
                nc.gpsimd.iota(all_rows[:, 0:NT, C], pattern=[[P, NT]], base=0, channel_multiplier=1,
                               allow_small_or_imprecise_dtypes=True).then_inc(noded, 1)
                pool.wait_ge(noded, 1)
                pool.wait_ge(kept, NT)
                pool.wait_ge(slots_ready, 1)
                for c, slot in enumerate(plan["slot"]):
                    if c == 1:
                        pool.wait_ge(scattered, 16 * NT)
                        nc.gpsimd.tensor_copy(all_rows[:, 0:NT, C + 1], gate2[:, :]).then_inc(noded, 1)
                        pool.wait_ge(noded, 2)
                    for t in range(NT):
                        n = P if t < NT - 1 else LAST
                        nc.gpsimd.indirect_dma_start(
                            xs_dram, bass.IndirectOffsetOnAxis(ap=slot[0:n, t:t + 1], axis=0),
                            all_rows[0:n, t, :], None).then_inc(scattered, 16)
                pool.wait_ge(scattered, 32 * NT)

            @block.scalar
            def _(act):
                act.wait_ge(sqrt_in, 1)
                nc.scalar.activation(var[:, :], var[:, :], ACT.Sqrt).then_inc(sqrt_done, 1)

                act.wait_ge(spilled, 48)

                def copy(t, b):
                    act.wait_ge(normed, t + 1)
                    nc.scalar.activation(x_rows[:, ds(t, 1), :].rearrange("p a c -> p (a c)"),
                                         hrow[b][:, :], ACT.Copy).then_inc(kept, 1)
                    act.wait_ge(transposed, t + 1)
                    if not early(t):
                        act.wait_ge(logit_done, t - 1)
                    nc.scalar.activation(hT[b][:, :], tp[b][:, 0:C], ACT.Copy).then_inc(turned, 1)
                over_tiles(act, copy)
                act.wait_ge(exp_in, 1)
                nc.scalar.activation(flat(l2), flat(l2), ACT.Exp).then_inc(exp_done, 1)
                nc.scalar.activation(m2[:, :], m2[:, :], ACT.Exp).then_inc(exp_done, 1)

                def high(n, turn, b):
                    act.wait_ge(wf_loaded[b], 16 * turn + 16)
                    nc.scalar.activation(w[:, ds(n * PIECE, PIECE)], wst[b][:, :], ACT.Copy).then_inc(wf_hi, 1)
                over_pieces(act, high)

            @block.vector
            def _(dve):
                v = nc.vector
                link = chained(dve, chain)
                for t in range(NT):
                    last = v.bn_stats(stats[:, t, :], x_rows[:, t, :])
                link(last)
                row_stats(nc, link, stats, mean, var, tmp)
                v.tensor_copy(tmp[:, :], var[:, :]).then_inc(sqrt_in, 1)
                dve.wait_ge(sqrt_done, 1)
                link(v.reciprocal(var[:, :], var[:, :]))

                def normalise(t, b):
                    if not early(t):
                        dve.wait_ge(transposed, t - 1)
                        dve.wait_ge(kept, t - 1)
                    row = x_rows[:, ds(t, 1), :].rearrange("p a c -> p (a c)")
                    v.tensor_scalar(hrow[b][:, :], row, mean[:, ds(t, 1)], var[:, ds(t, 1)],
                                    ALU.subtract, ALU.mult).then_inc(normed, 1)
                over_tiles(dve, normalise)

                def first_of(choice, values, top):
                    link(v.tensor_reduce(top[:, :], values[:, :, :], AX.X, ALU.max))
                    link(v.tensor_tensor(tm[:, :, :], values[:, :, :], wide(top), ALU.is_equal))
                    link(v.tensor_tensor(tm[:, :, :], tm[:, :, :],
                                         cst["first_wins"][:, :].unsqueeze(1).to_broadcast([P, NT, N_EXP]), ALU.mult))
                    link(v.tensor_reduce(wm[:, :], tm[:, :, :], AX.X, ALU.max))
                    link(v.tensor_tensor(choice[:, :, :], tm[:, :, :], wide(wm), ALU.is_equal))

                dve.wait_ge(logit_done, NT)
                dve.wait_ge(kept, NT)
                link(v.tensor_copy(flat(lg), lg_ps[:, 0:NE]))
                first_of(s1, lg, m1)
                link(v.scalar_tensor_tensor(out=flat(l2), in0=flat(s1), scalar=-3e38, in1=flat(lg),
                                            op0=ALU.mult, op1=ALU.add))
                first_of(s2, l2, m2)
                link(v.tensor_tensor(l2[:, :, :], lg[:, :, :], wide(m1), ALU.subtract))
                v.tensor_tensor(m2[:, :], m2[:, :], m1[:, :], ALU.subtract).then_inc(exp_in, 1)
                link(v.tensor_tensor(tm[:, :, :], s1[:, :, :], s2[:, :, :], ALU.add))
                v.tensor_tensor(both[:, :, :], tm[:, :, :],
                                wide(cst["valid"]), ALU.mult).then_inc(both_ready, 1)
                dve.wait_ge(exp_done, 2)
                link(v.tensor_reduce(ssum[:, :], l2[:, :, :], AX.X, ALU.add))
                link(v.reciprocal(ssum[:, :], ssum[:, :]))
                link(v.tensor_tensor(m2[:, :], m2[:, :], ssum[:, :], ALU.mult))
                link(v.tensor_tensor(m1[:, :], m2[:, :], ssum[:, :], ALU.add))
                link(v.tensor_scalar(m1[:, :], m1[:, :], 1e-9, None, ALU.add))
                link(v.reciprocal(m1[:, :], m1[:, :]))
                link(v.tensor_scalar(m1[:, :], m1[:, :], 1.0 / HSCALE, None, ALU.mult))
                link(v.tensor_tensor(all_rows[:, 0:NT, C + 1], ssum[:, :], m1[:, :], ALU.mult))
                link(v.tensor_tensor(gate2[:, :], m2[:, :], m1[:, :], ALU.mult))

                def by_expert(t):
                    return flat(t).rearrange("p (e t) -> p e t", e=N_EXP)
                dve.wait_ge(ranked, 2)
                link(v.tensor_copy(by_expert(tm), tot_ps[:, 0:NE].rearrange("p (t e) -> p e t", e=N_EXP)))
                link(v.memset(flat(po), 1.0))
                link(v.memset(by_expert(po)[:, :, 0:1], 0.0))
                link(v.tensor_tensor_scan(flat(l2), flat(po), flat(tm), 0.0, ALU.mult, ALU.add))
                link(v.tensor_copy(cnt[:, :], by_expert(l2)[:, :, NT - 1]))
                link(v.tensor_scalar(cnt[:, :], cnt[:, :], float(TOK - 1), None, ALU.add))
                link(v.tensor_copy(cnti[:, :], cnt[:, :]))
                link(v.tensor_scalar(cnti[:, :], cnti[:, :], TOK.bit_length() - 1, None, ALU.arith_shift_right))
                link(v.tensor_copy(tiles[:, :], cnti[:, :]))
                link(v.memset(one8[:, :], 1.0))
                link(v.tensor_tensor_scan(tiles_in[:, :], one8[:, :], tiles[:, :], 0.0, ALU.mult, ALU.add))
                link(v.tensor_tensor(tiles[:, :], tiles_in[:, :], tiles[:, :], ALU.subtract))
                link(v.tensor_scalar(tiles[:, :], tiles[:, :], float(TOK), None, ALU.mult))
                link(v.tensor_tensor(flat(l2), flat(l2), flat(tm), ALU.subtract))
                link(v.tensor_tensor(by_expert(l2), by_expert(l2),
                                     tiles[:, :].unsqueeze(2).to_broadcast([P, N_EXP, NT]), ALU.add))
                link(v.tensor_tensor(po[:, :, :], rank_ps[:, 0:NE].rearrange("p (t e) -> p t e", e=N_EXP),
                                     by_expert(l2).rearrange("p e t -> p t e"), ALU.add))
                for choice, slot in zip((s1, s2), plan["slot"]):
                    link(v.tensor_tensor(tm[:, :, :], choice[:, :, :], po[:, :, :], ALU.mult))
                    link(v.tensor_reduce(wm[:, :], tm[:, :, :], AX.X, ALU.add))
                    link(v.tensor_copy(slot[:, :], wm[:, :]))
                v.engine_nop().then_inc(slots_ready, 1)
                link(v.tensor_scalar(exj[:, :], cst["slot_tile"][:, :], tiles_in[:, 0:1], None, ALU.is_ge))
                for e in range(1, N_EXP - 1):
                    link(v.scalar_tensor_tensor(out=exj[:, :], in0=cst["slot_tile"][:, :], scalar=tiles_in[:, e:e + 1],
                                                in1=exj[:, :], op0=ALU.is_ge, op1=ALU.add))
                link(v.tensor_scalar(exj[:, :], exj[:, :], float(WPE), None, ALU.mult))
                link(v.tensor_copy(plan["weights_at"][:, :], exj[:, :]))

                def low(n, turn, b):
                    dve.wait_ge(wf_hi, n + 1)
                    v.tensor_tensor(w[:, ds(n * PIECE + W_LOW, PIECE)], wst[b][:, :], w[:, ds(n * PIECE, PIECE)],
                                    ALU.subtract).then_inc(wf_lo, 1)
                over_pieces(dve, low)

            @block.tensor
            def _(pe):
                def turn(t, b):
                    pe.wait_ge(normed, t + 1)
                    if not early(t):
                        pe.wait_ge(turned, t - 1)
                    for k in range(KC):
                        last = nc.tensor.transpose(tp[b][:, k * P:(k + 1) * P],
                                                   hrow[b][:, k * P:(k + 1) * P], cst["ident"][:, :])
                    last.then_inc(transposed, 1)

                def logits(t, b):
                    pe.wait_ge(turned, t + 1)
                    for k in range(KC):
                        last = nc.tensor.matmul(lg_ps[:, ds(t * N_EXP, N_EXP)], hT[b][:, k * P:(k + 1) * P],
                                                rw[:, k, :], start=(k == 0), stop=(k == KC - 1))
                    last.then_inc(logit_done, 1)

                pe.wait_ge(rw_loaded, 16)
                turn(0, 0)
                with pe.Fori(0, NT // 2) as i:
                    turn(2 * i + 1, 1)
                    logits(2 * i, 0)
                    turn(2 * i + 2, 0)
                    logits(2 * i + 1, 1)
                logits(NT - 1, 0)
                pe.wait_ge(both_ready, 1)
                nc.tensor.matmul(rank_ps[:, 0:NE], cst["lower"][:, :], flat(both),
                                 start=True, stop=True).then_inc(ranked, 1)
                nc.tensor.matmul(tot_ps[:, 0:NE], cst["ones"][:, :], flat(both),
                                 start=True, stop=True).then_inc(ranked, 1)


def experts(nc, cst, plan, w, room, xs_dram, out):
    ctx = ExitStack()
    with ctx:
        def sem(name):
            return ctx.enter_context(nc.semaphore(name))

        TT = TOK // P
        taken = [0]

        def sb(name, shape, dt=F32):
            size = 1
            for n in shape[1:]:
                size *= n
            words = size if dt == F32 else size // 2
            part = room[:, taken[0]:taken[0] + words]
            taken[0] += words
            if dt != F32:
                part = part.bitcast(dt)
            if len(shape) == 3:
                part = part.rearrange("p (a b) -> p a b", a=shape[1])
            return part

        xt = [sb(f"slot_rows{b}", [P, TT, CW]) for b in range(2)]
        nodes = sb("slot_nodes", [P, TT * NJ]).bitcast(I32)
        gates = sb("slot_gates", [P, TT * NJ])
        index = [sb(f"add_index{b}", [P, TT]).bitcast(I32) for b in range(2)]
        token = sb("token", [P, 1])
        xhi = [sb(f"s_hi{b}", [P, KC, TOK], F16) for b in range(2)]
        xlo = [sb(f"s_lo{b}", [P, KC, TOK], F16) for b in range(2)]
        silu = [sb(f"silu{b}", [P, TOK]) for b in range(2)]
        hid = [sb(f"hidden{b}", [P, TOK]) for b in range(2)]
        hhi = [sb(f"h_hi{b}", [P, NM, TOK], F16) for b in range(2)]
        hlo = [sb(f"h_lo{b}", [P, HM, TOK], F16) for b in range(2)]
        ys = [sb(f"y_rows{b}", [P, TT, C]) for b in range(2)]
        ring = [ctx.enter_context(nc.psum_tensor(f"h13_{b}", [P, 512], F32)) for b in range(4)]
        tp = ctx.enter_context(nc.psum_tensor("slot_T", [P, KC, TOK], F32))
        yp = [ctx.enter_context(nc.psum_tensor(f"y_ps{b}", [P, TT, C], F32)) for b in range(2)]

        loaded = [sem(f"slots_loaded{b}") for b in range(2)]
        added, taken_out, index_ready = sem("y_added"), sem("slots_read"), sem("add_index_ready")
        turned, xhi_ready, xlo_ready = sem("slots_turned"), sem("slots_hi"), sem("slots_lo")
        grp, silu_ready, mul_done = sem("h13_done"), sem("silu_ready"), sem("mul_done")
        hhi_ready, hlo_ready = sem("h_hi_ready"), sem("h_lo_ready")
        y_done, y_out = sem("y_done"), sem("y_out")

        def over_tiles(eng, body):
            for j in range(4):
                body(j, j // 2, j % 2, True)
            with eng.Fori(2, NJ // 2 - 1) as i:
                body(2 * i, i, 0, True)
                body(2 * i + 1, i, 1, True)
            body(NJ - 2, NJ // 2 - 1, 0, True)
            body(NJ - 1, NJ // 2 - 1, 1, False)

        def early(n, below=2):
            return isinstance(n, int) and n < below

        def part(m):
            return P if m < HM else 64

        with nc.Block() as block:
            @block.sync
            def _(sp):
                def load(j, half, b):
                    if not early(j):
                        sp.wait_ge(taken_out, 2 * (j - 1))
                    sp.dma_start(xt[b][:, :, :], xs_dram[ds(j * TOK, TOK), :].rearrange("(a p) c -> p a c", p=P)
                                 ).then_inc(loaded[b], 16)

                def body(j, half, b, follow):
                    if follow:
                        load(j + 1, half + b, 1 - b)
                load(0, 0, 0)
                over_tiles(sp, body)

            @block.gpsimd
            def _(pool):
                g = nc.gpsimd

                def take(j, half, b):
                    pool.wait_ge(turned, j + 1)
                    g.tensor_copy(nodes[:, ds(j * TT, TT)], xt[b][:, :, C]).then_inc(taken_out, 1)
                    g.tensor_copy(gates[:, ds(j * TT, TT)], xt[b][:, :, C + 1]).then_inc(taken_out, 1)

                def add(j, b):
                    pool.wait_ge(taken_out, 2 * (j + 1))
                    g.tensor_copy(index[b][:, :], nodes[:, ds(j * TT, TT)]).then_inc(index_ready, 1)
                    pool.wait_ge(index_ready, j + 1)
                    pool.wait_ge(y_out, TT * (j + 1))
                    if not early(j, 1):
                        pool.wait_ge(added, 16 * TT * j)
                    g.tensor_tensor(token[:, :], gates[:, 0:1], gates[:, 0:1], ALU.add)
                    for a in range(TT):
                        g.indirect_dma_start(out, bass.IndirectOffsetOnAxis(ap=index[b][:, a:a + 1], axis=0),
                                             ys[b][:, a, :], None, compute_op=ALU.add).then_inc(added, 16)

                def body(j, half, b, follow):
                    if follow:
                        take(j + 1, half + b, 1 - b)
                    if not early(j):
                        add(j - 2, b)
                take(0, 0, 0)
                over_tiles(pool, body)
                add(NJ - 2, 0)
                add(NJ - 1, 1)
                pool.wait_ge(added, 16 * TT * NJ)

            @block.scalar
            def _(act):
                a = nc.scalar.activation

                def x_high(j, half, b):
                    act.wait_ge(turned, j + 1)
                    if not early(j):
                        act.wait_ge(grp, NM * (j - 1))
                    a(xhi[b][:, :, :], tp[:, :, :], ACT.Copy).then_inc(xhi_ready, 1)

                def y_copy(j, half, b):
                    act.wait_ge(y_done, j + 1)
                    if not early(j):
                        act.wait_ge(added, 16 * TT * (j - 1))
                    act.wait_ge(taken_out, 2 * (j + 1))
                    for h in range(TT):
                        a(ys[b][:, h, :], yp[b][:, h, :], ACT.Copy,
                          scale=gates[:, ds(j * TT + h, 1)]).then_inc(y_out, 1)

                def h_high(j, m, b):
                    act.wait_ge(mul_done, NM * j + m + 1)
                    if m == 0 and not early(j):
                        act.wait_ge(y_done, j - 1)
                    n = part(m)
                    a(hhi[b][0:n, m, :], hid[m % 2][0:n, :], ACT.Copy).then_inc(hhi_ready, 1)

                def body(j, half, b, follow):
                    for m in range(NM):
                        n = part(m)
                        act.wait_ge(grp, NM * j + m + 1)
                        if not (early(j, 1) and m < 2):
                            act.wait_ge(mul_done, NM * j + m - 1)
                        a(silu[m % 2][0:n, :], ring[(NM * b + m) % 4][0:n, 0:TOK], ACT.Silu).then_inc(silu_ready, 1)
                        if m > 0:
                            h_high(j, m - 1, b)
                        if m == 1 and not early(j):
                            y_copy(j - 2, half - 1, b)
                        if m == 3 and follow:
                            x_high(j + 1, half + b, 1 - b)
                    h_high(j, NM - 1, b)
                x_high(0, 0, 0)
                over_tiles(act, body)
                y_copy(NJ - 2, NJ // 2 - 1, 0)
                y_copy(NJ - 1, NJ // 2 - 1, 1)

            @block.vector
            def _(dve):
                v = nc.vector
                def x_low(j, b):
                    dve.wait_ge(xhi_ready, j + 1)
                    v.tensor_tensor(xlo[b][:, :, :], tp[:, :, :], xhi[b][:, :, :], ALU.subtract).then_inc(xlo_ready, 1)

                def h_low(j, m, b):
                    dve.wait_ge(hhi_ready, NM * j + m + 1)
                    n = part(m)
                    low = hlo[b][:, m, :] if m < HM else hhi[b][64:P, m, :]
                    v.tensor_tensor(low, hid[m % 2][0:n, :], hhi[b][0:n, m, :],
                                    ALU.subtract).then_inc(hlo_ready, 1)

                def body(j, half, b, follow):
                    for m in range(NM):
                        n = part(m)
                        dve.wait_ge(silu_ready, NM * j + m + 1)
                        if not (early(j, 1) and m < 2):
                            dve.wait_ge(hlo_ready, NM * j + m - 1)
                        bank = ring[(NM * b + m) % 4]
                        h3 = bank[:, TOK:2 * TOK] if m < HM else bank[64:P, 0:TOK]
                        v.scalar_tensor_tensor(out=hid[m % 2][0:n, :], in0=silu[m % 2][0:n, :], scalar=HSCALE,
                                               in1=h3, op0=ALU.mult, op1=ALU.mult).then_inc(mul_done, 1)
                        if m > 0:
                            h_low(j, m - 1, b)
                        if m == 3 and follow:
                            x_low(j + 1, 1 - b)
                    h_low(j, NM - 1, b)
                x_low(0, 0)
                over_tiles(dve, body)

            @block.tensor
            def _(pe):
                mm = nc.tensor.matmul

                def turn(j, half, b):
                    pe.wait_ge(loaded[b], 16 * half + 16)
                    if not early(j, 1):
                        pe.wait_ge(xlo_ready, j)
                    for k in range(KC):
                        for a in range(TT):
                            last = nc.tensor.transpose(tp[:, k, a * P:(a + 1) * P],
                                                       xt[b][:, a, k * P:(k + 1) * P], cst["ident"][:, :])
                    last.then_inc(turned, 1)

                def hidden(j, m, b, at):
                    if not (early(j, 1) and m < 4):
                        pe.wait_ge(mul_done, NM * j + m - 3)
                    for u in range(2 if m < HM else 1):
                        out = ring[(NM * b + m) % 4][:, u * TOK:(u + 1) * TOK]
                        c0 = (2 * m + u) * P
                        n = 0
                        for k in range(KC):
                            hi = w[:, ds(at + (k * W13 + c0), P)]
                            lo = w[:, ds(at + (W_LOW + k * W13 + c0), P)]
                            for weights, x in ((hi, xhi), (hi, xlo), (lo, xhi)):
                                last = mm(out, weights, x[b][:, k, :], start=(n == 0), stop=(n == 3 * KC - 1))
                                n += 1
                    last.then_inc(grp, 1)

                def project(j, b, at):
                    pe.wait_ge(hlo_ready, NM * (j + 1))
                    if not early(j):
                        pe.wait_ge(y_out, TT * (j - 1))
                    for a in range(TT):
                        s = slice(a * P, (a + 1) * P)
                        for m in range(NM):
                            r = part(m)
                            hi = w[:, ds(at + (KC * W13 + m * C), C)]
                            lo = w[0:r, ds(at + (W_LOW + KC * W13 + m * C), C)]
                            mm(yp[b][:, a, :], hhi[b][0:r, m, s], lo, start=(m == 0), stop=False)
                            last = mm(yp[b][:, a, :], hhi[b][:, m, s], hi, start=False, stop=(m == HM))
                            if m < HM:
                                mm(yp[b][:, a, :], hlo[b][:, m, s], hi, start=False, stop=False)
                    last.then_inc(y_done, 1)

                def weights_at(j):
                    return pe.value_load(plan["weights_at"][0:1, ds(j, 1)], min_val=0, max_val=(N_EXP - 1) * WPE)

                def body(j, half, b, follow):
                    at = weights_at(j)
                    pe.wait_ge(xlo_ready, j + 1)
                    for m in range(NM):
                        hidden(j, m, b, at)
                        if m == 2 and follow:
                            turn(j + 1, half + b, 1 - b)
                    if not early(j, 1):
                        project(j - 1, 1 - b, weights_at(j - 1))
                turn(0, 0, 0)
                over_tiles(pe, body)
                project(NJ - 1, 1, weights_at(NJ - 1))


def gnn_then_experts(nc, x, src, dst, rel, norm, gnn_w, router, w_in, out):
    table = nc.dram_tensor("rel_table", [N_RELS * NPAD, C], F32).ap()
    xs_dram = nc.dram_tensor("slot_inputs", [SLOTS, CW], F32).ap()
    with ExitStack() as ctx:
        def sb(name, shape, dt=F32):
            return ctx.enter_context(nc.sbuf_tensor(name, shape, dt))
        all_rows = sb("x_rows", [P, NT + 1, CW])
        plan = {"slot": [sb(f"slot_of{c}", [P, NT], I32) for c in range(2)],
                "weights_at": sb("weights_at", [P, NJ], I32)}
        with ExitStack() as edge_ctx:
            def eb(name, shape, dt):
                return edge_ctx.enter_context(nc.sbuf_tensor(name, shape, dt))
            cst = constants(nc, ctx, edge_ctx)
            edges = {"row": eb("edge_row", [P, NCH * EPT], I32), "dst": eb("edge_dst", [P, NCH * EPT], F32),
                     "norm": eb("edge_norm", [P, NCH * EPT], F32),
                     "step_begin": eb("step_begin", [P, NCH], I32), "step_end": eb("step_end", [P, NCH], I32),
                     "tile_of_step": eb("tile_of_step", [P, NCH], I32),
                     "steps_past": eb("steps_past", [P, 1], I32), "window": eb("window", [P, NCH], I32),
                     "meta": eb("edge_meta", [P, NCH * 2 * EPT], F32)}
            transform(nc, cst, all_rows[:, 0:NT, 0:C], edges, x, gnn_w, src, dst, rel, norm, table)
            aggregate(nc, cst, all_rows[:, :, 0:C], edges, table, xs_dram)
            aggregate_past(nc, cst, all_rows[:, :, 0:C], edges, table)
        with nc.sbuf_tensor("expert_w", [P, 2 * W_LOW], F16) as w:
            route(nc, cst, all_rows, plan, w, out, xs_dram, router, w_in)
            experts(nc, cst, plan, w, all_rows[:, :, :].rearrange("p t c -> p (t c)"), xs_dram, out)


def kernel(x, src, dst, edge_type_16, edge_weight1, L0_gnn_weight, L0_ffn_router_w, L0_ffn_w1, L0_ffn_w2,
           L0_ffn_w3):
    import numpy as np
    import concourse.bacc as bacc
    from concourse.bass_utils import run_bass_kernel_spmd

    def edges_by_partition(a, pad):
        flat = np.full(NCH * CHUNK, pad, a.dtype)
        flat[:N_EDGES] = np.asarray(a).reshape(-1)
        return np.ascontiguousarray(flat.reshape(NCH, P, EPT).transpose(1, 0, 2).reshape(P, NCH * EPT))

    x, gnn, router = np.asarray(x), np.asarray(L0_gnn_weight), np.asarray(L0_ffn_router_w)
    w1, w2, w3 = (np.asarray(a) for a in (L0_ffn_w1, L0_ffn_w2, L0_ffn_w3))
    x_pad = np.zeros((NPAD, C), x.dtype)
    x_pad[:N_NODES] = x
    w13 = np.zeros((N_EXP, KC, P, W13), w1.dtype)
    for of, u in ((w1, 0), (w3, 1)):
        t = of.transpose(0, 2, 1).reshape(N_EXP, KC, P, H)
        for m in range(HM):
            w13[..., (2 * m + u) * P:(2 * m + u + 1) * P] = t[..., m * P:(m + 1) * P]
        w13[..., 2 * HM * P + 64 * u:2 * HM * P + 64 * u + HT] = t[..., HM * P:]
    w13 = w13.transpose(2, 0, 1, 3).reshape(P, N_EXP, KC * W13)
    w2p = np.zeros((N_EXP, NM * P, C), w2.dtype)
    w2p[:, :H] = w2.transpose(0, 2, 1)
    w2p[:, HM * P + 64:HM * P + 64 + HT] = w2p[:, HM * P:H]
    w2p = w2p.reshape(N_EXP, NM, P, C).transpose(2, 0, 1, 3).reshape(P, N_EXP, W2)
    arrays = {
        "x": x_pad,
        "src": edges_by_partition(np.asarray(src), 0),
        "dst": edges_by_partition(np.asarray(dst), N_NODES - 1),
        "rel": edges_by_partition(np.asarray(edge_type_16), 0),
        "norm": edges_by_partition(np.asarray(edge_weight1), 0),
        "gnn_w": np.ascontiguousarray(gnn),
        "router": np.ascontiguousarray(router.T.reshape(KC, P, N_EXP).transpose(1, 0, 2)),
        "experts": np.concatenate([w13, w2p], axis=2).reshape(P, N_EXP * WPE),
    }
    nc = bacc.Bacc("TRN2", target_bir_lowering=False, num_devices=1)
    aps = {n: nc.dram_tensor(n, a.shape, mybir.dt.from_np(a.dtype), kind="ExternalInput").ap()
           for n, a in arrays.items()}
    out = nc.dram_tensor("out", (NPAD + TOK, C), F32, kind="ExternalOutput").ap()
    gnn_then_experts(nc, *aps.values(), out)
    r = run_bass_kernel_spmd(nc, [arrays], core_ids=[0])
    return r.results[0]["out"][:N_NODES]
```
